# Optimizing a Trainium2 kernel written in Bass

```python
import numpy as np
import jax
import jax.numpy as jnp

def _softmax(x, axis=-1):
    return jax.nn.softmax(x, axis=axis)

def _gelu(x):
    return jax.nn.gelu(x, approximate=True)

def _silu(x):
    return jax.nn.silu(x)

def _sigmoid(x):
    return jax.nn.sigmoid(x)

def _layernorm(x, axis=-1, eps=1e-05):
    m = jnp.mean(x, axis=axis, keepdims=True)
    v = jnp.var(x, axis=axis, keepdims=True)
    return (x - m) / jnp.sqrt(v + eps)

def _scatter_add(tgt, idx, src, axis=0):
    return tgt.at[idx].add(src)

def _segment_sum(src, seg, n):
    return jax.ops.segment_sum(src, seg, n)
kernel_name = 'mk_seq_preln_d1_jaxref_r8_7d34bc'

def setup_inputs(seed: int=0):
    np.random.seed(seed)
    _w = jnp.asarray

    def _L0_attn_setup():
        import jax, jax.numpy as jnp
        import numpy as np
        key = jax.random.key(seed)
        k1, k2, k3 = jax.random.split(key, 3)
        N, S, D = (8, 256, 128)
        x = jax.random.normal(k1, (N, S, D), dtype=jnp.float32)
        std = np.sqrt(2.0 / D).astype(np.float32)
        w_lhs = jax.random.normal(k2, (1, 1, D), dtype=jnp.float32) * std
        w_rhs = jax.random.normal(k3, (1, 1, D), dtype=jnp.float32) * std
        return {'x': x, 'w_lhs': w_lhs, 'w_rhs': w_rhs}
    _L0_attn_in = _L0_attn_setup()

    def _L0_ffn_setup():
        import math
        import jax, jax.numpy as jnp
        import numpy as np
        TOP_K = 2
        _GELU_C = math.sqrt(2.0 / math.pi)

        def gelu_new(x):
            return 0.5 * x * (1.0 + jnp.tanh(_GELU_C * (x + 0.044715 * x * x * x)))
        key = jax.random.key(seed)
        ks = jax.random.split(key, 6)
        B, T, C, E, H = (2, 256, 128, 8, 512)
        s_in = 1.0 / math.sqrt(C)
        s_hid = 1.0 / math.sqrt(H)
        return {'x': jax.random.normal(ks[0], (B, T, C), dtype=jnp.float32), 'router_w': jax.random.normal(ks[1], (E, C), dtype=jnp.float32) * s_in, 'w_fc': jax.random.normal(ks[2], (E, C, H), dtype=jnp.float32) * s_in, 'b_fc': jax.random.normal(ks[3], (E, H), dtype=jnp.float32) * 0.02, 'w_proj': jax.random.normal(ks[4], (E, H, C), dtype=jnp.float32) * s_hid, 'b_proj': jax.random.normal(ks[5], (E, C), dtype=jnp.float32) * 0.02}
    _L0_ffn_in = _L0_ffn_setup()
    _d = {'L0_attn_x': _L0_attn_in['x'], 'L0_attn_w_lhs': _L0_attn_in['w_lhs'], 'L0_attn_w_rhs': _L0_attn_in['w_rhs'], 'L0_ffn_router_w': _L0_ffn_in['router_w'], 'L0_ffn_w_fc': _L0_ffn_in['w_fc'], 'L0_ffn_b_fc': _L0_ffn_in['b_fc'], 'L0_ffn_w_proj': _L0_ffn_in['w_proj'], 'L0_ffn_b_proj': _L0_ffn_in['b_proj']}
    _x0 = _d['L0_attn_x']
    _d['L0_attn_x'] = jax.random.normal(jax.random.fold_in(jax.random.key(seed), 1), (4, 1024, 128), dtype=_x0.dtype)
    del _x0
    return _d

def reference(L0_attn_x, L0_attn_w_lhs, L0_attn_w_rhs, L0_ffn_router_w, L0_ffn_w_fc, L0_ffn_b_fc, L0_ffn_w_proj, L0_ffn_b_proj):

    def _L0_attn_ref(x, w_lhs, w_rhs):
        import jax, jax.numpy as jnp
        import numpy as np
        lhs = x * w_lhs
        rhs = x * w_rhs
        scores = jnp.einsum('nsd,ntd->nst', lhs, rhs)
        attn = jax.nn.softmax(scores, axis=2)
        return jnp.einsum('nst,ntd->nsd', attn, x)

    def _L0_ffn_ref(x, router_w, w_fc, b_fc, w_proj, b_proj):
        import math
        import jax, jax.numpy as jnp
        import numpy as np
        TOP_K = 2
        _GELU_C = math.sqrt(2.0 / math.pi)

        def gelu_new(x):
            return 0.5 * x * (1.0 + jnp.tanh(_GELU_C * (x + 0.044715 * x * x * x)))
        B, T, C = x.shape
        E = router_w.shape[0]
        N = B * T
        xf = x.reshape(N, C)
        logits = xf @ router_w.T
        probs = jax.nn.softmax(logits, axis=-1)
        topk_probs, topk_idx = jax.lax.top_k(probs, TOP_K)
        topk_probs = topk_probs / jnp.sum(topk_probs, axis=-1, keepdims=True)
        combine = jnp.zeros((N, E), dtype=x.dtype).at[jnp.arange(N)[:, None], topk_idx].add(topk_probs)
        h = gelu_new(jnp.einsum('nc,ech->neh', xf, w_fc) + b_fc)
        out = jnp.einsum('neh,ehc->nec', h, w_proj) + b_proj
        y = jnp.einsum('nec,ne->nc', out, combine)
        return y.reshape(B, T, C)
    x = L0_attn_x
    x = x + _L0_attn_ref(_layernorm(x, axis=-1), L0_attn_w_lhs, L0_attn_w_rhs)
    x = x + _L0_ffn_ref(_layernorm(x, axis=-1), L0_ffn_router_w, L0_ffn_w_fc, L0_ffn_b_fc, L0_ffn_w_proj, L0_ffn_b_proj)
    return x

_drawn_inputs = setup_inputs


def setup_inputs(seed=0):
    import zlib

    import numpy as np

    out = dict(_drawn_inputs(seed))
    spreads = {}
    factors = {'L0_ffn_b_fc': 6.116, 'L0_ffn_b_proj': 4.093}
    for name, (base, spread) in spreads.items():
        noise = np.random.default_rng([zlib.crc32(name.encode()), seed]).standard_normal(out[name].shape)
        drawn = base * np.exp(spread * noise) if base else spread * noise
        out[name] = jnp.asarray(drawn.astype(out[name].dtype))
    for name, factor in factors.items():
        out[name] = (out[name] * factor).astype(out[name].dtype)
    return out
```

```python
from contextlib import ExitStack

import concourse.bass as bass
from concourse import mybir

P = 128
F32 = mybir.dt.float32
F32R = mybir.dt.float32r
F16 = mybir.dt.float16
U32 = mybir.dt.uint32
ALU = mybir.AluOpType
ACT = mybir.ActivationFunctionType
AX_X = mybir.AxisListType.X
RMAX = bass.bass_isa.ReduceOp.max
EPS = 1e-5
TOP = 2.0 ** 14


def preln_attention_moe(nc, x, w_lhs, w_rhs, router_wT, w_fc, b_fc, w_proj, b_proj, out):
    NT = x.shape[1]
    D = x.shape[2]
    E = router_wT.shape[1]
    HID = w_fc.shape[2]
    HC = HID // P
    B = 4
    BT = NT // B
    S = BT * P
    GT = 4
    NG = NT // GT
    GN = GT * P
    assert D == P and NT % (B * 8) == 0 and E == 8

    with ExitStack() as ctx:
        def sb(name, shape, dt):
            return ctx.enter_context(nc.sbuf_tensor(name, shape, dt))

        def sem(name):
            return ctx.enter_context(nc.semaphore(name))

        res = sb("res", [P, NT, D], F32)
        h_parts = sb("h_parts", [P, NT, 2 * D], F16)
        h_tile = sb("h_tile", [P, BT, D], F32)
        hT = sb("hT", [P, NT * P], F32)
        hT_hi = sb("hT_hi", [P, NT * P], F32R)
        hT_lo = sb("hT_lo", [P, NT * P], F32R)
        q = sb("q", [P, 2, P], F32)
        q_hi = sb("q_hi", [P, 2, P], F32R)
        q_lo = sb("q_lo", [P, 2, P], F32R)
        prob = sb("prob", [P, 2, S], F32)
        prob_hi = sb("prob_hi", [P, 2, S], F16)
        prob_lo = sb("prob_lo", [P, 2, S], F16)
        probT_hi = sb("probT_hi", [P, 2, S], F16)
        probT_lo = sb("probT_lo", [P, 2, S], F16)
        neg_max = sb("neg_max", [P, 2], F32)
        row_sum = sb("row_sum", [P, NT], F32)
        inv_sum = sb("inv_sum", [P, 2], F32)
        att = sb("att", [P, 2, D], F32)
        w_d = sb("w_d", [P, 3], F32)
        ident = sb("ident", [P, P], F32)
        ident16 = sb("ident16", [P, P], F16)
        stats = sb("stats", [P, BT, 6], F32)
        moments = sb("moments", [P, BT, 2], F32)
        var_eps = sb("var_eps", [P, NT], F32)
        rstd = sb("rstd", [P, NT], F32)
        moments2 = sb("moments2", [P, NT, 2], F32)
        minus_half = sb("minus_half", [P, NT], F32)

        h2T_hi = sb("h2T_hi", [P, NT * P], F16)
        h2T_lo = sb("h2T_lo", [P, NT * P], F16)
        wfc_hi = sb("wfc_hi", [P, E, HID], F16)
        wfc_lo = sb("wfc_lo", [P, E, HID], F16)
        wpr_hi = sb("wpr_hi", [P, E, HC, D], F16)
        wpr_lo = sb("wpr_lo", [P, E, HC, D], F16)
        wraw = prob[:, :, :].rearrange("p a s -> p (a s)")
        bfc = sb("bfc", [P, E, HC], F32)
        bpr = sb("bpr", [E, D], F32)
        rwT = sb("rwT", [P, E], F32)
        peak = sb("peak", [P, 4], F32)
        peaks = sb("peaks", [P, 4], F32)
        pow2 = sb("pow2", [P, 3], F32)
        scale_up = sb("scale_up", [P, 3], F32)
        scale_down = sb("scale_down", [P, 4], F32)
        logits = sb("logits", [P, NT, E], F32)
        top_logit = sb("top_logit", [P, NT, 2], F32)
        first_id = sb("first_id", [P, NT], F32)
        expert_id = sb("expert_id", [P, NT, E], F32)
        gate2 = sb("gate2", [P, NT], F32)
        gate_sum = sb("gate_sum", [P, NT], F32)
        gates = sb("gates", [P, NT, 2], F32)
        pick = sb("pick", [P, NT, E], F32)
        pick2 = sb("pick2", [P, NT, E], F32)
        combine = sb("combine", [P, NT, E], F32)
        combine_s = sb("combine_s", [P, NT, E], F32)
        comb_g = sb("comb_g", [P, GT, E], F32)
        combT = sb("combT", [E, 2, GN], F32)
        hid = hT[:, :].rearrange("p (a c n) -> p a c n", a=2, c=HC)
        hid_hi = h_parts[:, 0:NT // 2, :].rearrange("p t d -> p (t d)").rearrange(
            "p (a c n) -> p a c n", a=2, c=HC)
        hid_lo = h_parts[:, NT // 2:NT, :].rearrange("p t d -> p (t d)").rearrange(
            "p (a c n) -> p a c n", a=2, c=HC)

        bank = [ctx.enter_context(nc.psum_tensor(f"bank{i}", [P, 512], F32)) for i in range(2)]
        sc_ps = ctx.enter_context(nc.psum_tensor("sc_ps", [P, 4, 512], F32))
        av_ps = ctx.enter_context(nc.psum_tensor("av_ps", [P, 2, 512], F32))
        scores = [sc_ps[:, 2 * a:2 * a + 2, :].rearrange("p a n -> p (a n)") for a in range(2)]
        turn_hi = bank[0][:, :].bitcast(F16)
        turn_lo = bank[1][:, :].bitcast(F16)

        x_in = [sem(f"x_in{i}") for i in range(B)]
        small_in = sem("small_in")
        w_in = sem("w_in")
        wfc_in = sem("wfc_in")
        wpr_in = sem("wpr_in")
        consts = sem("consts")
        stats_made = sem("stats_made")
        moments_made = sem("moments_made")
        var_made = sem("var_made")
        rstd_made = sem("rstd_made")
        h_made = sem("h_made")
        hhi_made = sem("hhi_made")
        hlo_made = sem("hlo_made")
        h_turned = sem("h_turned")
        hT_made = sem("hT_made")
        hThi_made = sem("hThi_made")
        hTlo_made = sem("hTlo_made")
        w_made = sem("w_made")
        q_made = sem("q_made")
        qhi_made = sem("qhi_made")
        qlo_made = sem("qlo_made")
        scored = sem("scored")
        max_made = sem("max_made")
        prob_made = sem("prob_made")
        phi_made = sem("phi_made")
        plo_made = sem("plo_made")
        hi_turned = sem("hi_turned")
        lo_turned = sem("lo_turned")
        pThi_made = sem("pThi_made")
        pTlo_made = sem("pTlo_made")
        attended = sem("attended")
        inv_made = sem("inv_made")
        att_made = sem("att_made")
        res_made = sem("res_made")
        ln2_stats = sem("ln2_stats")
        ln2_moments = sem("ln2_moments")
        ln2_kept = sem("ln2_kept")
        ln2_var = sem("ln2_var")
        ln2_rstd = sem("ln2_rstd")
        h2_made = sem("h2_made")
        h2_turned = sem("h2_turned")
        h2T_made = sem("h2T_made")
        h2hi_made = sem("h2hi_made")
        h2lo_made = sem("h2lo_made")
        routed = sem("routed")
        logits_out = sem("logits_out")
        gap_made = sem("gap_made")
        waited_apart = sem("waited_apart")
        peak_made = sem("peak_made")
        peaks_made = sem("peaks_made")
        dve_chain = sem("dve_chain")
        gate_exp = sem("gate_exp")
        w_split = sem("w_split")
        comb_made = sem("comb_made")
        comb_turned = sem("comb_turned")
        combT_made = sem("combT_made")
        bias_mixed = sem("bias_mixed")
        bias_added = sem("bias_added")
        fc_done = sem("fc_done")
        gelu_done = sem("gelu_done")
        split_hi = sem("split_hi")
        hid_split = sem("hid_split")
        proj_done = sem("proj_done")
        mixed = sem("mixed")
        stored = sem("stored")

        def par(u):
            return u % 2 if isinstance(u, int) else None

        block = ctx.enter_context(nc.Block())

        STEADY = (2, NT - 4)

        def run_steps(eng, step):
            for u in range(STEADY[0]):
                step(u, u % 2)
            with eng.Fori(STEADY[0], STEADY[1], 2) as u:
                step(u, 0)
                step(u + 1, 1)
            for u in range(STEADY[1], NT):
                step(u, u % 2)

        def peeled(eng, count, body):
            body(0)
            with eng.Fori(1, count) as i:
                body(i)

        def wait_apart(eng, sem, value):
            eng.wait_ge(sem, value)
            eng.sem_inc(waited_apart, 1)

        def later(i, least=1):
            return not isinstance(i, int) or i >= least

        def there(u):
            return not isinstance(u, int) or 0 <= u < NT

        @block.sync
        def _(sp):
            sp.dma_start(w_d[:, 0:1], w_lhs).then_inc(w_in, 16)
            sp.dma_start(w_d[:, 1:2], w_rhs).then_inc(w_in, 16)
            for b in range(B):
                sp.dma_start(res[:, b * BT:(b + 1) * BT, :], x[:, b * BT:(b + 1) * BT, :]).then_inc(x_in[b], 16)
            sp.dma_start(rwT[:, :], router_wT).then_inc(small_in, 16)
            sp.dma_start(bfc[:, :, :], b_fc).then_inc(small_in, 16)
            sp.dma_start(bpr[:, :], b_proj).then_inc(small_in, 16)
            sp.wait_ge(att_made, NT)
            sp.dma_start(hT[:, :], w_fc.rearrange("c e h -> c (e h)")).then_inc(wfc_in, 16)
            sp.dma_start(h_parts[:, :, :].bitcast(F32).rearrange("p t d -> p (t d)"), w_proj.rearrange("p e c d -> p (e c d)")).then_inc(wpr_in, 16)
            with sp.Fori(0, NG) as g:
                sp.wait_ge(mixed, (g + 1) * E)
                sp.dma_start(out[:, bass.ds(g * GT, GT), :], res[:, bass.ds(g * GT, GT), :]).then_inc(stored, 16)
            sp.wait_ge(stored, 16 * NG)

        @block.gpsimd
        def _(pool):
            for m in (ident, ident16):
                pool.memset(m[:, :], 0.0).then_inc(consts, 1)
            pool.memset(minus_half[:, :], -0.5).then_inc(consts, 1)
            pool.iota(expert_id[:, :, :], pattern=[[0, NT], [1, E]], base=0, channel_multiplier=0,
                      allow_small_or_imprecise_dtypes=True).then_inc(consts, 1)
            pool.wait_ge(consts, 2)
            for m in (ident, ident16):
                pool.affine_select(out=m[:, :], in_=m[:, :], compare_op=ALU.not_equal, fill=1.0,
                                   base=0, pattern=[[-1, P]], channel_multiplier=1).then_inc(consts, 1)
            pool.wait_ge(consts, 6)
            def one_batch(b):
                pool.wait_ge(var_made, b + 1)
                pool.tensor_tensor(rstd[:, 0:BT], var_eps[:, 0:BT], minus_half[:, 0:BT], ALU.pow).then_inc(rstd_made, 1)
            peeled(pool, B, one_batch)

            def step(u, a):
                v = u + 1
                if there(v):
                    if later(v, 2):
                        pool.wait_ge(lo_turned, v - 1)
                    pool.wait_ge(phi_made, v + 1)
                    a = 1 - a
                    pool.tensor_tensor(prob_lo[:, a, :], prob[:, a, :], prob_hi[:, a, :], ALU.subtract).then_inc(plo_made, 1)
            step(-1, 1)
            run_steps(pool, step)
            pool.wait_ge(ln2_kept, NT)
            pool.tensor_scalar(var_eps[:, :], moments2[:, :, 1], EPS, 1.0, ALU.add, ALU.mult).then_inc(ln2_var, 1)
            pool.wait_ge(ln2_var, 1)
            pool.tensor_tensor(rstd[:, :], var_eps[:, :], minus_half[:, :], ALU.pow).then_inc(ln2_rstd, 1)
            pool.wait_ge(peak_made, 3)
            pool.partition_all_reduce(peaks[:, 0:3], peak[:, 0:3], P, RMAX).then_inc(peaks_made, 1)

        @block.scalar
        def _(act):
            def one_batch(b):
                at = bass.ds(b * BT, BT)
                cols = bass.ds(b * S, S)
                act.wait_ge(h_made, (b + 1) * BT)
                act.activation(h_parts[:, at, 0:D], h_tile[:, :, :], ACT.Copy).then_inc(hhi_made, 1)
                act.wait_ge(h_turned, b + 1)
                act.activation(hT[:, cols], scores[0], ACT.Copy).then_inc(hT_made, 1)
                act.activation(hT_hi[:, cols], scores[0], ACT.Copy).then_inc(hThi_made, 1)
            peeled(act, B, one_batch)
            act.wait_ge(w_made, 1)
            act.wait_ge(hT_made, B)

            def make_q(v, a):
                if later(v, 2):
                    act.wait_ge(scored, v - 1)
                    act.wait_ge(qlo_made, v - 1)
                cols = bass.ds(v * P, P)
                act.activation(q[:, a, :], hT[:, cols], ACT.Copy, scale=w_d[:, 2:3]).then_inc(q_made, 1)
                act.activation(q_hi[:, a, :], hT[:, cols], ACT.Copy, scale=w_d[:, 2:3]).then_inc(qhi_made, 1)

            def make_prob(v, a):
                act.wait_ge(max_made, v + 1)
                if later(v, 2):
                    act.wait_ge(plo_made, v - 1)
                    act.wait_ge(hi_turned, v - 1)
                act.activation(prob[:, a, :], scores[a], ACT.Exp, bias=neg_max[:, a:a + 1],
                               accum_out=row_sum[:, bass.ds(v, 1)]).then_inc(prob_made, 1)
                act.activation(prob_hi[:, a, :], scores[a], ACT.Exp, bias=neg_max[:, a:a + 1]).then_inc(phi_made, 1)

            def step(u, a):
                if there(u + 3):
                    make_q(u + 3, 1 - a)
                act.wait_ge(hi_turned, u + 1)
                if later(u, 2):
                    act.wait_ge(attended, u - 1)
                act.activation(probT_hi[:, a, :], turn_hi, ACT.Copy).then_inc(pThi_made, 1)
                if there(u + 2):
                    make_prob(u + 2, a)

            make_q(0, 0)
            make_q(1, 1)
            make_prob(0, 0)
            make_q(2, 0)
            make_prob(1, 1)
            run_steps(act, step)

            def one_group(g):
                act.wait_ge(h2_turned, g + 1)
                cols = bass.ds(g * GN, GN)
                if later(g):
                    act.wait_ge(routed, g)
                act.activation(prob[:, 0, 0:GN], av_ps[:, 0, :], ACT.Copy).then_inc(h2T_made, 1)
                act.activation(h2T_hi[:, cols], av_ps[:, 0, :], ACT.Copy).then_inc(h2hi_made, 1)
            peeled(act, NG, one_group)
            act.wait_ge(gap_made, 1)
            act.activation(gate2[:, :], gate_sum[:, :], ACT.Exp).then_inc(gate_exp, 1)
            def one_group(g):
                act.wait_ge(comb_turned, g + 1)
                if later(g):
                    act.wait_ge(bias_mixed, g)
                act.activation(combT[:, 0, :], bank[0][0:E, :], ACT.Copy).then_inc(combT_made, 1)
            peeled(act, NG, one_group)

            act.wait_ge(small_in, 48)
            act.wait_ge(w_split, 4)
            for e in range(E):
                hidden_first = e < 2
                for c in range(HC):
                    act.wait_ge(fc_done, e * HC + c + 1)
                    if not hidden_first and c == 0:
                        act.wait_ge(hid_split, (e - 1) * HC)
                    act.activation(hid[:, e % 2, c, :], sc_ps[:, c, :], ACT.Gelu_apprx_tanh,
                                   bias=bfc[:, e, c:c + 1], scale=scale_down[:, 0:1]).then_inc(gelu_done, 1)
            with act.Fori(1, NG) as g:
                for e in range(E):
                    i = g * E + e
                    for c in range(HC):
                        act.wait_ge(fc_done, i * HC + c + 1)
                        if c == 0:
                            act.wait_ge(hid_split, (i - 1) * HC)
                        act.activation(hid[:, e % 2, c, :], sc_ps[:, c, :], ACT.Gelu_apprx_tanh,
                                       bias=bfc[:, e, c:c + 1], scale=scale_down[:, 0:1]).then_inc(gelu_done, 1)

        @block.tensor
        def _(pe):
            pe.wait_ge(consts, 6)
            def one_batch(b):
                pe.wait_ge(h_made, (b + 1) * BT)
                if later(b):
                    pe.wait_ge(hThi_made, b)
                for t in range(BT):
                    mm = pe.transpose(scores[0][:, t * P:(t + 1) * P], h_tile[:, t, :], ident[:, :])
                mm.then_inc(h_turned, 1)
            peeled(pe, B, one_batch)
            pe.wait_ge(hThi_made, B)
            pe.wait_ge(hTlo_made, B)

            def score(v, a):
                pe.wait_ge(qhi_made, v + 1)
                pe.wait_ge(qlo_made, v + 1)
                if later(v, 2):
                    pe.wait_ge(phi_made, v - 1)
                first = (v // BT) * S
                for n in range(S // 512):
                    cols = bass.ds(first + n * 512, 512)
                    o = scores[a][:, n * 512:(n + 1) * 512]
                    pe.matmul(o, q_hi[:, a, :], hT_hi[:, cols], start=True, stop=False)
                    pe.matmul(o, q_hi[:, a, :], hT_lo[:, cols], start=False, stop=False)
                    mm = pe.matmul(o, q_lo[:, a, :], hT_hi[:, cols], start=False, stop=True)
                mm.then_inc(scored, 1)

            def turn(u, a):
                for parts, to, made, copied, turned in ((prob_hi, turn_hi, phi_made, pThi_made, hi_turned),
                                                        (prob_lo, turn_lo, plo_made, pTlo_made, lo_turned)):
                    pe.wait_ge(made, u + 1)
                    if later(u):
                        pe.wait_ge(copied, u)
                    for t in range(BT):
                        mm = pe.transpose(to[:, t * P:(t + 1) * P], parts[:, a, t * P:(t + 1) * P], ident16[:, :])
                    mm.then_inc(turned, 1)

            def attend(v, a):
                pe.wait_ge(pThi_made, v + 1)
                pe.wait_ge(pTlo_made, v + 1)
                if later(v, 2):
                    pe.wait_ge(att_made, v - 1)
                first = (v // BT) * BT
                for t in range(BT):
                    pe.matmul(av_ps[:, a, 0:2 * D], probT_hi[:, a, t * P:(t + 1) * P], h_parts[:, first + t, :],
                              start=(t == 0), stop=False, skip_group_check=True)
                    mm = pe.matmul(av_ps[:, a, 0:D], probT_lo[:, a, t * P:(t + 1) * P], h_parts[:, first + t, 0:D],
                                   start=False, stop=(t == BT - 1), skip_group_check=True)
                mm.then_inc(attended, 1)

            def step(u, a):
                if there(u + 2):
                    score(u + 2, a)
                turn(u, a)
                if later(u):
                    attend(u - 1, 1 - a)

            pe.wait_ge(hlo_made, B)
            score(0, 0)
            score(1, 1)
            run_steps(pe, step)
            attend(NT - 1, 1)

            pe.wait_ge(small_in, 48)
            def one_group(g):
                pe.wait_ge(h2_made, (g + 1) * GT)
                if later(g):
                    pe.wait_ge(h2lo_made, g)
                for t in range(GT):
                    mm = pe.transpose(av_ps[:, 0, t * P:(t + 1) * P], h_tile[:, t, :], ident[:, :])
                mm.then_inc(h2_turned, 1)
                pe.wait_ge(h2T_made, g + 1)
                if later(g):
                    pe.wait_ge(logits_out, g)
                for t in range(GT):
                    mm = pe.matmul(av_ps[:, 1, t * E:(t + 1) * E], prob[:, 0, t * P:(t + 1) * P], rwT[:, :],
                                   start=True, stop=True)
                mm.then_inc(routed, 1)
            peeled(pe, NG, one_group)
            def one_group(g):
                if later(g):
                    pe.wait_ge(combT_made, g)
                pe.wait_ge(comb_made, g + 1)
                for t in range(GT):
                    mm = pe.transpose(bank[0][0:E, t * P:(t + 1) * P], comb_g[:, t, :], ident[:, :])
                mm.then_inc(comb_turned, 1)
                pe.wait_ge(combT_made, g + 1)
                if later(g):
                    pe.wait_ge(bias_added, g)
                for t in range(GT):
                    mm = pe.matmul(bank[1][:, t * D:(t + 1) * D], combT[:, 0, t * P:(t + 1) * P], bpr[:, :],
                                   start=True, stop=True)
                mm.then_inc(bias_mixed, 1)
            peeled(pe, NG, one_group)
            pe.wait_ge(w_split, 4)
            pe.wait_ge(h2lo_made, NG)
            pe.wait_ge(h2hi_made, NG)
            pe.wait_ge(bias_added, NG)

            def up(g, e, i):
                cols = bass.ds(g * GN, GN)
                for c in range(HC):
                    if later(i):
                        pe.wait_ge(gelu_done, (i - 1) * HC + c + 1)
                    w = slice(c * P, (c + 1) * P)
                    pe.matmul(sc_ps[:, c, :], wfc_hi[:, e, w], h2T_hi[:, cols], start=True, stop=False)
                    pe.matmul(sc_ps[:, c, :], wfc_hi[:, e, w], h2T_lo[:, cols], start=False, stop=False)
                    pe.matmul(sc_ps[:, c, :], wfc_lo[:, e, w], h2T_hi[:, cols], start=False, stop=True).then_inc(fc_done, 1)

            out_ps = [bank[0][:, :], bank[1][:, :]]

            def down(e, i, a):
                pe.wait_ge(hid_split, (i + 1) * HC)
                if later(i, 2):
                    pe.wait_ge(mixed, i - 1)
                for t in range(GT):
                    o = out_ps[a][:, t * D:(t + 1) * D]
                    for c in range(HC):
                        hi = hid_hi[:, a, c, t * P:(t + 1) * P]
                        lo = hid_lo[:, a, c, t * P:(t + 1) * P]
                        pe.matmul(o, hi, wpr_hi[:, e, c, :], start=(c == 0), stop=False, skip_group_check=True)
                        pe.matmul(o, hi, wpr_lo[:, e, c, :], start=False, stop=False, skip_group_check=True)
                        mm = pe.matmul(o, lo, wpr_hi[:, e, c, :], start=False, stop=(c == HC - 1), skip_group_check=True)
                mm.then_inc(proj_done, 1)

            up(0, 0, 0)
            for e in range(1, E):
                up(0, e, e)
                down(e - 1, e - 1, (e - 1) % 2)
            with pe.Fori(1, NG) as g:
                for e in range(E):
                    i = g * E + e
                    up(g, e, i)
                    down((e - 1) % E, i - 1, (e - 1) % 2)
            down(E - 1, NG * E - 1, 1)

        @block.vector
        def _(dve):
            dve.wait_ge(w_in, 32)
            dve.tensor_tensor(w_d[:, 2:3], w_d[:, 0:1], w_d[:, 1:2], ALU.mult).then_inc(w_made, 1)
            for b in range(B):
                dve.wait_ge(x_in[b], 16)
            def one_batch(b):
                for t in range(BT):
                    ins = dve.bn_stats(stats[:, t, :], res[:, b * BT + t, :])
                ins.then_inc(stats_made, 1)
                wait_apart(dve, stats_made, b + 1)
                for t in range(BT):
                    ins = dve.bn_aggr(moments[:, t, :], stats[:, t, :])
                ins.then_inc(moments_made, 1)
                dve.wait_ge(moments_made, b + 1)
                dve.tensor_scalar(var_eps[:, 0:BT], moments[:, :, 1], EPS, None, ALU.add).then_inc(var_made, 1)
                dve.wait_ge(rstd_made, b + 1)
                if later(b):
                    dve.wait_ge(h_turned, b)
                if later(b):
                    dve.wait_ge(hhi_made, b)
                if later(b):
                    dve.wait_ge(hlo_made, b)
                for t in range(BT):
                    n = b * BT + t
                    dve.tensor_scalar(h_tile[:, t, :], res[:, n, :], moments[:, t, 0:1], rstd[:, t:t + 1],
                                      ALU.subtract, ALU.mult).then_inc(h_made, 1)
                at = bass.ds(b * BT, BT)
                cols = bass.ds(b * S, S)
                dve.wait_ge(hhi_made, b + 1)
                dve.wait_ge(h_made, (b + 1) * BT)
                dve.tensor_tensor(h_parts[:, at, D:2 * D], h_tile[:, :, :], h_parts[:, at, 0:D], ALU.subtract).then_inc(hlo_made, 1)
                dve.wait_ge(hThi_made, b + 1)
                dve.tensor_tensor(hT_lo[:, cols], hT[:, cols], hT_hi[:, cols].bitcast(F32), ALU.subtract).then_inc(hTlo_made, 1)
            peeled(dve, B, one_batch)

            def split_q(v, a):
                dve.wait_ge(qhi_made, v + 1)
                dve.tensor_tensor(q_lo[:, a, :], q[:, a, :], q_hi[:, a, :].bitcast(F32), ALU.subtract).then_inc(qlo_made, 1)

            def row_max(v, a):
                dve.wait_ge(scored, v + 1)
                if later(v, 2):
                    dve.wait_ge(phi_made, v - 1)
                dve.tensor_reduce(neg_max[:, a:a + 1], scores[a], AX_X, ALU.max, negate=True).then_inc(max_made, 1)

            def finish(v, a):
                dve.wait_ge(prob_made, v + 1)
                dve.reciprocal(inv_sum[:, a:a + 1], row_sum[:, bass.ds(v, 1)]).then_inc(inv_made, 1)
                dve.wait_ge(inv_made, v + 1)
                dve.wait_ge(attended, v + 1)
                dve.scalar_tensor_tensor(out=att[:, a, :], in0=av_ps[:, a, 0:D], scalar=inv_sum[:, a:a + 1],
                                         in1=res[:, v, :], op0=ALU.mult, op1=ALU.add).then_inc(res_made, 1)
                dve.wait_ge(res_made, v + 1)
                dve.scalar_tensor_tensor(out=res[:, v, :], in0=av_ps[:, a, D:2 * D], scalar=inv_sum[:, a:a + 1],
                                         in1=att[:, a, :], op0=ALU.mult, op1=ALU.add).then_inc(att_made, 1)
                wait_apart(dve, att_made, v + 1)
                dve.bn_stats(stats[:, a, :], res[:, v, :]).then_inc(ln2_stats, 1)
                wait_apart(dve, ln2_stats, v + 1)
                dve.bn_aggr(moments[:, a, :], stats[:, a, :]).then_inc(ln2_moments, 1)
                dve.wait_ge(ln2_moments, v + 1)
                dve.tensor_copy(moments2[:, v, :], moments[:, a, :]).then_inc(ln2_kept, 1)

            def step(u, a):
                if there(u + 3):
                    split_q(u + 3, 1 - a)
                if there(u + 2):
                    row_max(u + 2, a)
                dve.wait_ge(lo_turned, u + 1)
                if later(u, 2):
                    dve.wait_ge(attended, u - 1)
                dve.tensor_copy(probT_lo[:, a, :].bitcast(F32), turn_lo.bitcast(F32)).then_inc(pTlo_made, 1)
                if later(u):
                    finish(u - 1, 1 - a)

            split_q(0, 0)
            split_q(1, 1)
            row_max(0, 0)
            split_q(2, 0)
            row_max(1, 1)
            run_steps(dve, step)
            finish(NT - 1, 1)

            dve.wait_ge(ln2_rstd, 1)
            def one_group(g):
                if later(g):
                    dve.wait_ge(h2_turned, g)
                for t in range(GT):
                    n = g * GT + t
                    dve.tensor_scalar(h_tile[:, t, :], res[:, n, :], moments2[:, n, 0:1], rstd[:, bass.ds(n, 1)],
                                      ALU.subtract, ALU.mult).then_inc(h2_made, 1)
                cols = bass.ds(g * GN, GN)
                dve.wait_ge(h2hi_made, g + 1)
                dve.tensor_tensor(h2T_lo[:, cols], av_ps[:, 0, :], h2T_hi[:, cols], ALU.subtract).then_inc(h2lo_made, 1)
                dve.wait_ge(routed, g + 1)
                at = bass.ds(g * GT, GT)
                dve.tensor_copy(logits[:, at, :], av_ps[:, 1, 0:GT * E].rearrange("p (t e) -> p t e", e=E)).then_inc(logits_out, 1)

            peeled(dve, NG, one_group)

            chain = [0]

            def link(ins):
                chain[0] += 1
                ins.then_inc(dve_chain, 1)
                dve.wait_ge(dve_chain, chain[0])

            def bc(ap):
                return ap.unsqueeze(2).to_broadcast([P, NT, E])

            dve.wait_ge(logits_out, NG)
            dve.wait_ge(consts, 6)
            for k, p in ((0, pick), (1, pick2)):
                best = top_logit[:, :, k]
                link(dve.tensor_reduce(best, logits[:, :, :], AX_X, ALU.max))
                link(dve.tensor_tensor(p[:, :, :], logits[:, :, :], bc(best), ALU.is_equal))
                link(dve.scalar_tensor_tensor(out=p[:, :, :], in0=p[:, :, :], scalar=-2.0 * E, in1=expert_id[:, :, :],
                                              op0=ALU.mult, op1=ALU.add))
                link(dve.tensor_reduce(first_id[:, :], p[:, :, :], AX_X, ALU.min))
                link(dve.tensor_tensor(p[:, :, :], p[:, :, :], bc(first_id[:, :]), ALU.is_equal))
                if k == 0:
                    link(dve.scalar_tensor_tensor(out=logits[:, :, :], in0=p[:, :, :], scalar=-3e38, in1=logits[:, :, :],
                                                  op0=ALU.mult, op1=ALU.add))
            dve.tensor_tensor(gate_sum[:, :], top_logit[:, :, 1], top_logit[:, :, 0], ALU.subtract).then_inc(gap_made, 1)
            dve.wait_ge(gate_exp, 1)
            link(dve.tensor_scalar(gate_sum[:, :], gate2[:, :], 1.0, None, ALU.add))
            link(dve.reciprocal(gates[:, :, 0], gate_sum[:, :]))
            link(dve.tensor_tensor(gates[:, :, 1], gates[:, :, 0], gate2[:, :], ALU.mult))
            for k, p in ((0, pick), (1, pick2)):
                link(dve.tensor_tensor(p[:, :, :], p[:, :, :], bc(gates[:, :, k]), ALU.mult))
            link(dve.tensor_tensor(combine[:, :, :], pick[:, :, :], pick2[:, :, :], ALU.add))
            dve.wait_ge(small_in, 48)
            dve.wait_ge(wfc_in, 16)
            dve.tensor_reduce(peak[:, 0:1], hT[:, :], AX_X, ALU.max, apply_absolute_value=True).then_inc(peak_made, 1)
            dve.wait_ge(wpr_in, 16)
            raw_proj = h_parts[:, :, :].bitcast(F32).rearrange("p t d -> p (t d)")
            dve.tensor_reduce(peak[:, 1:2], raw_proj, AX_X, ALU.max, apply_absolute_value=True).then_inc(peak_made, 1)
            dve.tensor_reduce(peak[:, 2:3], bfc[:, :, :].rearrange("p e c -> p (e c)"), AX_X, ALU.max,
                              apply_absolute_value=True).then_inc(peak_made, 1)
            dve.wait_ge(peaks_made, 1)
            link(dve.scalar_tensor_tensor(out=peaks[:, 2:3], in0=peaks[:, 0:1], scalar=float(D) ** 0.5 * D * 1.01,
                                          in1=peaks[:, 2:3], op0=ALU.mult, op1=ALU.add))
            link(dve.tensor_scalar(peaks[:, 0:3], peaks[:, 0:3], 2.0 ** -90, 2.0 ** 100, ALU.max, ALU.min))
            link(dve.tensor_scalar(pow2[:, :].bitcast(U32), peaks[:, 0:3].bitcast(U32), 0x7F800000, None, ALU.bitwise_and))
            link(dve.reciprocal(scale_up[:, :], pow2[:, :]))
            link(dve.tensor_scalar(scale_up[:, :], scale_up[:, :], TOP, None, ALU.mult))
            link(dve.tensor_scalar(scale_down[:, 0:3], pow2[:, :], 1.0 / TOP, None, ALU.mult))
            link(dve.tensor_tensor(scale_down[:, 3:4], scale_down[:, 1:2], scale_down[:, 2:3], ALU.mult))
            link(dve.tensor_scalar(combine_s[:, :, :], combine[:, :, :], scale_down[:, 3:4], None, ALU.mult))
            for k, raw, hi, lo in ((0, hT[:, :], wfc_hi[:, :, :].rearrange("p e h -> p (e h)"), wfc_lo[:, :, :].rearrange("p e h -> p (e h)")),
                                   (1, raw_proj, wpr_hi[:, :, :, :].rearrange("p e c d -> p (e c d)"), wpr_lo[:, :, :, :].rearrange("p e c d -> p (e c d)"))):
                dve.tensor_scalar(hi, raw, scale_up[:, k:k + 1], None, ALU.mult).then_inc(w_split, 1)
                dve.wait_ge(w_split, 2 * k + 1)
                dve.scalar_tensor_tensor(out=lo, in0=raw, scalar=scale_up[:, k:k + 1], in1=hi,
                                         op0=ALU.mult, op1=ALU.subtract).then_inc(w_split, 1)
            def one_group(g):
                at = bass.ds(g * GT, GT)
                if later(g):
                    dve.wait_ge(comb_turned, g)
                dve.tensor_copy(comb_g[:, :, :], combine[:, at, :]).then_inc(comb_made, 1)
                dve.wait_ge(bias_mixed, g + 1)
                dve.tensor_tensor(res[:, at, :], res[:, at, :], bank[1][:, :].rearrange("p (t d) -> p t d", d=D), ALU.add).then_inc(bias_added, 1)
            peeled(dve, NG, one_group)
            dve.wait_ge(bias_added, NG)
            dve.wait_ge(w_split, 4)

            def split_hidden(i, a):
                for c in range(HC):
                    dve.wait_ge(gelu_done, i * HC + c + 1)
                    if c == 0 and (later(i, 2)):
                        dve.wait_ge(proj_done, i - 1)
                    dve.tensor_scalar(hid_hi[:, a, c, :], hid[:, a, c, :], scale_up[:, 2:3], None, ALU.mult).then_inc(split_hi, 1)
                    dve.wait_ge(split_hi, i * HC + c + 1)
                    dve.scalar_tensor_tensor(out=hid_lo[:, a, c, :], in0=hid[:, a, c, :], scalar=scale_up[:, 2:3],
                                             in1=hid_hi[:, a, c, :], op0=ALU.mult, op1=ALU.subtract).then_inc(hid_split, 1)

            def mix(g, e, i, a):
                dve.wait_ge(proj_done, i + 1)
                if later(i):
                    dve.wait_ge(mixed, i)
                for t in range(GT):
                    n = g * GT + t
                    o = bank[a][:, t * D:(t + 1) * D]
                    ins = dve.scalar_tensor_tensor(out=res[:, n, :], in0=o, scalar=combine_s[:, n, e:e + 1],
                                                   in1=res[:, n, :], op0=ALU.mult, op1=ALU.add)
                ins.then_inc(mixed, 1)

            split_hidden(0, 0)
            for e in range(1, E):
                split_hidden(e, e % 2)
                mix(0, e - 1, e - 1, (e - 1) % 2)
            with dve.Fori(1, NG) as g:
                split_hidden(g * E, 0)
                mix(g - 1, E - 1, g * E - 1, 1)
                for e in range(1, E):
                    split_hidden(g * E + e, e % 2)
                    mix(g, e - 1, g * E + e - 1, (e - 1) % 2)
            mix(NG - 1, E - 1, NG * E - 1, 1)


_INS = ['L0_attn_x', 'L0_attn_w_lhs', 'L0_attn_w_rhs', 'L0_ffn_router_w', 'L0_ffn_w_fc', 'L0_ffn_b_fc',
        'L0_ffn_w_proj', 'L0_ffn_b_proj']


def kernel(**inputs):
    import numpy as _np
    import concourse.bacc as _bacc
    from concourse import mybir as _mybir
    from concourse.bass_utils import run_bass_kernel_spmd as _run

    x, w_lhs, w_rhs, router_w, w_fc, b_fc, w_proj, b_proj = (_np.asarray(inputs[n]) for n in _INS)
    n_b, n_s, d = x.shape
    n_e, _, hid = w_fc.shape
    laid = {
        "x": x.reshape(n_b * n_s // 128, 128, d).transpose(1, 0, 2),
        "w_lhs": w_lhs.reshape(d, 1),
        "w_rhs": w_rhs.reshape(d, 1),
        "router_wT": router_w.T,
        "w_fc": w_fc.transpose(1, 0, 2),
        "b_fc": b_fc.reshape(n_e, hid // 128, 128).transpose(2, 0, 1),
        "w_proj": w_proj.reshape(n_e, hid // 128, 128, d).transpose(2, 0, 1, 3),
        "b_proj": b_proj,
    }
    nc = _bacc.Bacc("TRN2", target_bir_lowering=False, num_devices=1)
    arrays, args = {}, []
    for name, a in laid.items():
        a = _np.ascontiguousarray(a)
        arrays[f"in_{name}_dram"] = a
        args.append(nc.dram_tensor(f"in_{name}_dram", a.shape, _mybir.dt.from_np(a.dtype), kind="ExternalInput").ap())
    out = nc.dram_tensor("out_0_dram", laid["x"].shape, _mybir.dt.float32, kind="ExternalOutput").ap()
    preln_attention_moe(nc, *args, out)
    r = _run(nc, [arrays], core_ids=[0])
    got = r.results[0]["out_0_dram"]
    return _np.ascontiguousarray(got.transpose(1, 0, 2)).reshape(n_b, n_s, d)
```

```python
from contextlib import ExitStack

import concourse.bass as bass
from concourse import mybir

P = 128
F32 = mybir.dt.float32
F32R = mybir.dt.float32r
F16 = mybir.dt.float16
U32 = mybir.dt.uint32
I32 = mybir.dt.int32
ALU = mybir.AluOpType
ACT = mybir.ActivationFunctionType
AX_X = mybir.AxisListType.X
RMAX = bass.bass_isa.ReduceOp.max
EPS = 1e-5
TOP = 2.0 ** 14


def preln_attention_moe(nc, x, w_lhs, w_rhs, router_wT, w_fc, b_fc, w_proj, b_proj, out):
    NT = x.shape[1]
    D = x.shape[2]
    E = router_wT.shape[1]
    HID = w_fc.shape[2]
    HC = HID // P
    B = 4
    BT = NT // B
    S = BT * P
    N = NT * P
    K = 2
    ROW = D + 2
    H = 2
    W = H * P
    NB = 8
    NTILES = -(-((K * N + E * (W - 1)) // W) // NB) * NB
    NH = 4
    slots = nc.dram_tensor("slots", [E * N, ROW], F32, kind="Internal").ap()
    SPARE = K * N + E * W
    results = nc.dram_tensor("results", [SPARE + NTILES * W, D], F32, kind="Internal").ap()
    assert D == P and NT % (B * 8) == 0 and E == 8

    with ExitStack() as ctx:
        def sb(name, shape, dt):
            return ctx.enter_context(nc.sbuf_tensor(name, shape, dt))

        def sem(name):
            return ctx.enter_context(nc.semaphore(name))

        res = sb("res", [P, NT, D], F32)
        h_parts = sb("h_parts", [P, NT, 2 * D], F16)
        h_tile = sb("h_tile", [P, BT, D], F32)
        hT = sb("hT", [P, NT * P], F32)
        hT_hi = sb("hT_hi", [P, NT * P], F32R)
        hT_lo = sb("hT_lo", [P, NT * P], F32R)
        q = sb("q", [P, 2, P], F32)
        q_hi = sb("q_hi", [P, 2, P], F32R)
        q_lo = sb("q_lo", [P, 2, P], F32R)
        prob = sb("prob", [P, 2, S], F32)
        prob_hi = sb("prob_hi", [P, 2, S], F16)
        prob_lo = sb("prob_lo", [P, 2, S], F16)
        probT_hi = sb("probT_hi", [P, 2, S], F16)
        probT_lo = sb("probT_lo", [P, 2, S], F16)
        neg_max = sb("neg_max", [P, 2], F32)
        row_sum = sb("row_sum", [P, NT], F32)
        inv_sum = sb("inv_sum", [P, 2], F32)
        att = sb("att", [P, 2, D], F32)
        w_d = sb("w_d", [P, 3], F32)
        ident = sb("ident", [P, P], F32)
        ident16 = sb("ident16", [P, P], F16)
        stats = sb("stats", [P, BT, 6], F32)
        moments = sb("moments", [P, BT, 2], F32)
        var_eps = sb("var_eps", [P, NT], F32)
        rstd = sb("rstd", [P, NT], F32)
        var2 = sb("var2", [P, 2, 1], F32)
        rstd2 = sb("rstd2", [P, 2, 1], F32)
        minus_half = sb("minus_half", [P, NT], F32)

        h2 = sb("h2", [P, 2, D], F32)
        h2_parts = hT[:, :].bitcast(F16).rearrange("p (t d) -> p t d", d=2 * D)
        h2T = sb("h2T", [P, 2, P], F32)
        raw_fc = sb("raw_fc", [P, E * HID], F32)
        raw_proj = sb("raw_proj", [P, E * HID], F32)
        wfc_hi = sb("wfc_hi", [P, E, HID], F16)
        wfc_lo = sb("wfc_lo", [P, E, HID], F16)
        wpr = sb("wpr", [P, E, HC, 2 * D], F16)
        bfc = sb("bfc", [P, E, HC], F32)
        bpr = sb("bpr", [P, E, D], F32)
        rwT = sb("rwT", [P, E], F32)
        peak = sb("peak", [P, 4], F32)
        peaks = sb("peaks", [P, 4], F32)
        pow2 = sb("pow2", [P, 3], F32)
        scale_up = sb("scale_up", [P, 3], F32)
        scale_down = sb("scale_down", [P, 4], F32)
        logits = sb("logits", [P, NT, E], F32)
        best = sb("best", [P, BT, 2], F32)
        lg = sb("lg", [P, BT, E], F32)
        first_id = sb("first_id", [P, BT], F32)
        expert_id = sb("expert_id", [P, BT, E], F32)
        gap = sb("gap", [P, BT], F32)
        gate2 = sb("gate2", [P, BT], F32)
        gate_sum = sb("gate_sum", [P, BT], F32)
        gates = sb("gates", [P, BT, 2], F32)
        pick = [sb(f"pick{k}", [P, BT, E], F32) for k in range(K)]
        taken = sb("taken", [P, BT + 1, E], F16)
        rank = sb("rank", [P, BT, E], F32)
        rank_k = sb("rank_k", [P, BT, E], F32)
        slot_f = sb("slot_f", [P, BT, K], F32)
        slot = sb("slot", [P, NT, K], I32)
        next_slot = sb("next_slot", [P, E], F32)
        meta = sb("meta", [P, NT, K, 2], F32)
        before = sb("before", [P, P], F16)
        ones16 = sb("ones16", [P, P], F16)
        stage = [sb(f"stage{a}", [P, K, ROW], F32) for a in range(2)]
        stage_slot = [sb(f"stage_slot{a}", [P, K], I32) for a in range(2)]
        empty = raw_fc[:, 0:E * H * ROW].rearrange("p (e h r) -> p e h r", e=E, h=H)

        region = sb("region", [P, E], F32)
        count = sb("count", [P, E], F32)
        tiles_i = sb("tiles_i", [P, E], I32)
        tiles = sb("tiles", [P, E], F32)
        ends = [sb(f"ends{i}", [P, E], F32) for i in range(4)]
        last_row = sb("last_row", [P, E], F32)
        tile_id = sb("tile_id", [P, NTILES], F32)
        past = h_tile[:, :, :].rearrange("p t d -> p (t d)")[:, 0:NTILES * E].rearrange("p (k e) -> p k e", e=E)
        past2 = sb("past2", [P, NTILES, E], F32)
        expert_row = sb("expert_row", [P, NTILES, E], F32)
        of_expert = sb("of_expert", [P, NTILES], F32)
        tile_row = sb("tile_row", [P, NTILES], F32)
        tile_last = sb("tile_last", [P, NTILES], F32)
        tile_expert = sb("tile_expert", [P, NTILES], I32)
        tile_start = sb("tile_start", [P, NTILES], I32)
        skipped = sb("skipped", [P, NTILES], F32)
        place = sb("place", [P, H], F32)
        spare = sb("spare", [P, NTILES, H], F32)
        spare_row = sb("spare_row", [P, NTILES, H], F32)

        xs_all = raw_proj[:, 0:NB * H * ROW].rearrange("p (a h r) -> p a h r", a=NB, h=H)
        xs = [xs_all[:, a, :, :] for a in range(NB)]
        xT = sb("xT", [P, NH, 2 * W], F16)
        hid = raw_fc[:, :].rearrange("p (a c n) -> p a c n", a=NH, c=HC)
        hid_hi = h_parts[:, 0:NT // 2, :].rearrange("p t d -> p (t d)").rearrange("p (a c n) -> p a c n", a=NH, c=HC)
        hid_lo = h_parts[:, NT // 2:NT, :].rearrange("p t d -> p (t d)").rearrange("p (a c n) -> p a c n", a=NH, c=HC)
        biased = h_tile[:, :, :].rearrange("p t d -> p (t d)").rearrange("p (a h d) -> p a h d", a=NH, h=H)
        gated_all = prob[:, :, :].rearrange("p a s -> p (a s)").rearrange("p (a h d) -> p a h d", a=NB, h=H)
        gated = [[gated_all[:, a, h, :] for h in range(H)] for a in range(NB)]
        result_row = [sb(f"result_row{a}", [P, H], I32) for a in range(NB)]

        bank = [ctx.enter_context(nc.psum_tensor(f"bank{i}", [P, 512], F32)) for i in range(2)]
        sc_ps = ctx.enter_context(nc.psum_tensor("sc_ps", [P, 4, 512], F32))
        av_ps = ctx.enter_context(nc.psum_tensor("av_ps", [P, 2, 512], F32))
        scores = [sc_ps[:, 2 * a:2 * a + 2, :].rearrange("p a n -> p (a n)") for a in range(2)]
        turn_hi = bank[0][:, :].bitcast(F16)
        turn_lo = bank[1][:, :].bitcast(F16)

        x_in = [sem(f"x_in{i}") for i in range(B)]
        small_in = sem("small_in")
        w_in = sem("w_in")
        wfc_in = sem("wfc_in")
        wpr_in = sem("wpr_in")
        consts = sem("consts")
        stats_made = sem("stats_made")
        moments_made = sem("moments_made")
        var_made = sem("var_made")
        rstd_made = sem("rstd_made")
        h_made = sem("h_made")
        hhi_made = sem("hhi_made")
        hlo_made = sem("hlo_made")
        h_turned = sem("h_turned")
        hT_made = sem("hT_made")
        hThi_made = sem("hThi_made")
        hTlo_made = sem("hTlo_made")
        w_made = sem("w_made")
        q_made = sem("q_made")
        qhi_made = sem("qhi_made")
        qlo_made = sem("qlo_made")
        scored = sem("scored")
        max_made = sem("max_made")
        prob_made = sem("prob_made")
        phi_made = sem("phi_made")
        plo_made = sem("plo_made")
        hi_turned = sem("hi_turned")
        lo_turned = sem("lo_turned")
        pThi_made = sem("pThi_made")
        pTlo_made = sem("pTlo_made")
        attended = sem("attended")
        inv_made = sem("inv_made")
        att_made = sem("att_made")
        res_made = sem("res_made")
        ln2_stats = sem("ln2_stats")
        ln2_moments = sem("ln2_moments")
        ln2_var = sem("ln2_var")
        ln2_rstd = sem("ln2_rstd")
        h2_made = sem("h2_made")
        h2hi_made = sem("h2hi_made")
        h2lo_made = sem("h2lo_made")
        h2_turned = sem("h2_turned")
        h2T_made = sem("h2T_made")
        routed = sem("routed")
        logits_out = sem("logits_out")
        gap_made = sem("gap_made")
        waited_apart = sem("waited_apart")
        peak_made = sem("peak_made")
        peaks_made = sem("peaks_made")
        dve_chain = sem("dve_chain")
        route_chain = sem("route_chain")
        gate_exp = sem("gate_exp")
        w_split = sem("w_split")
        taken_made = sem("taken_made")
        ranked = sem("ranked")
        slots_made = sem("slots_made")
        empty_made = sem("empty_made")
        emptied = sem("emptied")
        stage_made = sem("stage_made")
        dispatched = [sem(f"dispatched{a}") for a in range(2)]
        table_made = sem("table_made")
        xs_in = [sem(f"xs_in{a}") for a in range(NB)]
        xs_turned = sem("xs_turned")
        xT_made = sem("xT_made")
        fc_done = sem("fc_done")
        gelu_done = sem("gelu_done")
        split_hi = sem("split_hi")
        hid_split = sem("hid_split")
        proj_done = sem("proj_done")
        bias_added = sem("bias_added")
        biased_made = sem("biased_made")
        gated_made = sem("gated_made")
        row_made = sem("row_made")
        returned = [sem(f"returned{a}") for a in range(NB)]
        results_in = [sem(f"results_in{b}") for b in range(B)]
        summed = sem("summed")
        added = sem("added")
        stored = sem("stored")

        def par(u):
            return u % 2 if isinstance(u, int) else None

        N_CONSTS = 15

        block = ctx.enter_context(nc.Block())

        STEADY = (4, NT - 4)

        def run_steps(eng, step):
            for u in range(STEADY[0]):
                step(u, u % 2)
            with eng.Fori(STEADY[0] // 2, STEADY[1] // 2) as i:
                step(2 * i, 0)
                step(2 * i + 1, 1)
            for u in range(STEADY[1], NT):
                step(u, u % 2)

        def peeled(eng, count, body):
            body(0)
            with eng.Fori(1, count) as i:
                body(i)

        def wait_apart(eng, sem, value):
            eng.wait_ge(sem, value)
            eng.sem_inc(waited_apart, 1)

        def later(i, least=1):
            return not isinstance(i, int) or i >= least

        def there(u):
            return not isinstance(u, int) or 0 <= u < NT

        def run_tiles(eng, step, lag):
            for k in range(NB):
                step(k, k)
            with eng.Fori(1, NTILES // NB) as i:
                for a in range(NB):
                    step(i * NB + a, a)
            for k in range(NTILES, NTILES + lag):
                step(k, k % NB)

        def run_tiles_ahead(eng, step, lag):
            for k in range(NB):
                step(k, k)
            with eng.Fori(1, NTILES // NB - 1) as i:
                for a in range(NB):
                    step(i * NB + a, a)
            for k in range(NTILES - NB, NTILES + lag):
                step(k, k % NB)

        def up_ps(a, c):
            return sc_ps[:, 2 * (a % 2) + c // 2, (c % 2) * W:(c % 2 + 1) * W]

        def tile_there(k):
            return not isinstance(k, int) or 0 <= k < NTILES

        @block.sync
        def _(sp):
            sp.dma_start(w_d[:, 0:1], w_lhs).then_inc(w_in, 16)
            sp.dma_start(w_d[:, 1:2], w_rhs).then_inc(w_in, 16)
            for b in range(B):
                sp.dma_start(res[:, b * BT:(b + 1) * BT, :], x[:, b * BT:(b + 1) * BT, :]).then_inc(x_in[b], 16)
            sp.dma_start(rwT[:, :], router_wT).then_inc(small_in, 16)
            sp.dma_start(bfc[:, :, :], b_fc).then_inc(small_in, 16)
            sp.dma_start(bpr[:, :, :], b_proj.unsqueeze(0).to_broadcast([P, E, D])).then_inc(small_in, 16)
            sp.dma_start(raw_fc[:, :], w_fc.rearrange("c e h -> c (e h)")).then_inc(wfc_in, 16)
            sp.dma_start(raw_proj[:, :], w_proj.rearrange("p e c d -> p (e c d)")).then_inc(wpr_in, 16)
            sp.wait_ge(empty_made, 2)
            sp.dma_start(slots.rearrange("(e n) r -> e n r", e=E)[:, 0:W, :].rearrange("e (p h) r -> p e (h r)", h=H),
                         empty.rearrange("p e h r -> p e (h r)")).then_inc(emptied, 16)

            for a in range(2):
                sp.wait_ge(dispatched[a], 16 * K * NT // 2)
            sp.wait_ge(table_made, 1)

            def load(k, a):
                start = sp.value_load(tile_start[0:1, bass.ds(k, 1)], min_val=0, max_val=E * N - W)
                if later(k, NB):
                    sp.wait_ge(returned[a], 16 * H * (k // NB))
                sp.dma_start(xs[a], slots[bass.ds(start, W), :].rearrange("(p h) r -> p h r", h=H)).then_inc(xs_in[a], 16)
            run_tiles(sp, load, 0)

            for a in range(NB):
                sp.wait_ge(returned[a], 16 * H * NTILES // NB)
            both = results[0:K * N, :].rearrange("(t p k) d -> p t (k d)", p=P, k=K)
            for b in range(B):
                half = (raw_fc, raw_proj)[b // 2][:, :].rearrange("p (t x) -> p t x", x=K * D)
                sp.dma_start(half[:, (b % 2) * BT:(b % 2 + 1) * BT, :], both[:, b * BT:(b + 1) * BT, :]).then_inc(results_in[b], 16)
            for b in range(B):
                sp.wait_ge(added, b + 1)
                sp.dma_start(out[:, b * BT:(b + 1) * BT, :], res[:, b * BT:(b + 1) * BT, :]).then_inc(stored, 16)
            sp.wait_ge(stored, 16 * B)

        @block.gpsimd
        def _(pool):
            for m in (ident, ident16):
                pool.memset(m[:, :], 0.0).then_inc(consts, 1)
            pool.memset(minus_half[:, :], -0.5).then_inc(consts, 1)
            pool.iota(expert_id[:, :, :], pattern=[[0, BT], [1, E]], base=0, channel_multiplier=0,
                      allow_small_or_imprecise_dtypes=True).then_inc(consts, 1)
            pool.iota(region[:, :], pattern=[[N, E]], base=0, channel_multiplier=0,
                      allow_small_or_imprecise_dtypes=True).then_inc(consts, 1)
            pool.iota(next_slot[:, :], pattern=[[N, E]], base=0, channel_multiplier=0,
                      allow_small_or_imprecise_dtypes=True).then_inc(consts, 1)
            pool.iota(meta[:, :, :, 0], pattern=[[K * P, NT], [1, K]], base=0, channel_multiplier=K,
                      allow_small_or_imprecise_dtypes=True).then_inc(consts, 1)
            pool.iota(tile_id[:, :], pattern=[[1, NTILES]], base=0, channel_multiplier=0,
                      allow_small_or_imprecise_dtypes=True).then_inc(consts, 1)
            pool.iota(place[:, :], pattern=[[1, H]], base=0, channel_multiplier=H,
                      allow_small_or_imprecise_dtypes=True).then_inc(consts, 1)
            pool.iota(spare[:, :, :], pattern=[[W, NTILES], [1, H]], base=SPARE, channel_multiplier=H,
                      allow_small_or_imprecise_dtypes=True).then_inc(consts, 1)
            pool.memset(taken[:, BT:BT + 1, :], 0.0).then_inc(consts, 1)
            pool.memset(ones16[:, :], 1.0).then_inc(consts, 1)
            pool.wait_ge(consts, N_CONSTS - 3)
            pool.affine_select(out=before[:, :], in_=ones16[:, :], compare_op=ALU.is_gt, fill=0.0,
                               base=0, pattern=[[1, P]], channel_multiplier=-1).then_inc(consts, 1)
            for m in (ident, ident16):
                pool.affine_select(out=m[:, :], in_=m[:, :], compare_op=ALU.not_equal, fill=1.0,
                                   base=0, pattern=[[-1, P]], channel_multiplier=1).then_inc(consts, 1)
            def one_batch(b):
                pool.wait_ge(var_made, b + 1)
                pool.tensor_tensor(rstd[:, 0:BT], var_eps[:, 0:BT], minus_half[:, 0:BT], ALU.pow).then_inc(rstd_made, 1)
            peeled(pool, B, one_batch)

            def split_q(v, a):
                pool.wait_ge(q_made, v + 1)
                pool.wait_ge(qhi_made, v + 1)
                if later(v, 2):
                    pool.wait_ge(scored, v - 1)
                pool.tensor_tensor(q_lo[:, a, :], q[:, a, :], q_hi[:, a, :].bitcast(F32), ALU.subtract).then_inc(qlo_made, 1)

            def scale_ln2(v, a):
                pool.wait_ge(ln2_var, v + 1)
                pool.tensor_tensor(rstd2[:, a, :], var2[:, a, :], minus_half[:, 0:1], ALU.pow).then_inc(ln2_rstd, 1)

            def split_h2(v, a):
                pool.wait_ge(h2hi_made, v + 1)
                pool.tensor_tensor(h2_parts[:, v, D:2 * D], h2[:, a, :], h2_parts[:, v, 0:D], ALU.subtract).then_inc(h2lo_made, 1)

            def step(u, a):
                if later(u, 2):
                    scale_ln2(u - 2, a)
                if later(u, 3):
                    split_h2(u - 3, 1 - a)
                v = u + 1
                if there(v):
                    if later(v, 2):
                        pool.wait_ge(lo_turned, v - 1)
                    pool.wait_ge(phi_made, v + 1)
                    o = 1 - a
                    pool.tensor_tensor(prob_lo[:, o, :], prob[:, o, :], prob_hi[:, o, :], ALU.subtract).then_inc(plo_made, 1)
                if later(u, 0) and there(u + 3):
                    split_q(u + 3, 1 - a)
            pool.wait_ge(peak_made, 3)
            pool.partition_all_reduce(peaks[:, 0:3], peak[:, 0:3], P, RMAX).then_inc(peaks_made, 1)
            pool.wait_ge(w_split, 2)
            pool.memset(empty, 0.0).then_inc(empty_made, 1)
            pool.wait_ge(empty_made, 1)
            pool.iota(empty[:, :, :, D], pattern=[[W, E], [1, H]], base=K * N, channel_multiplier=H,
                      allow_small_or_imprecise_dtypes=True).then_inc(empty_made, 1)
            for v in range(3):
                split_q(v, v % 2)
            step(-1, 1)
            run_steps(pool, step)
            scale_ln2(NT - 2, 0)
            split_h2(NT - 3, 1)
            scale_ln2(NT - 1, 1)
            split_h2(NT - 2, 0)
            split_h2(NT - 1, 1)

            pool.wait_ge(emptied, 16)

            def dispatch(n, a):
                wait_apart(pool, stage_made, 3 * (n + 1))
                for k in range(K):
                    pool.indirect_dma_start(out=slots[:, :], out_offset=bass.IndirectOffsetOnAxis(ap=stage_slot[a][:, k:k + 1], axis=0),
                                            in_=stage[a][:, k, :], in_offset=None).then_inc(dispatched[a], 16)
            with pool.Fori(0, NT // 2) as i:
                dispatch(2 * i, 0)
                dispatch(2 * i + 1, 1)

            def give_back(k, a):
                pool.wait_ge(row_made, k + 1)
                wait_apart(pool, gated_made, k + 1)
                for h in range(H):
                    pool.indirect_dma_start(out=results[:, :], out_offset=bass.IndirectOffsetOnAxis(ap=result_row[a][:, h:h + 1], axis=0),
                                            in_=gated[a][h], in_offset=None).then_inc(returned[a], 16)
            run_tiles(pool, give_back, 0)

        @block.scalar
        def _(act):
            def one_batch(b):
                at = bass.ds(b * BT, BT)
                cols = bass.ds(b * S, S)
                act.wait_ge(h_made, (b + 1) * BT)
                act.activation(h_parts[:, at, 0:D], h_tile[:, :, :], ACT.Copy).then_inc(hhi_made, 1)
                act.wait_ge(h_turned, b + 1)
                act.activation(hT[:, cols], scores[0], ACT.Copy).then_inc(hT_made, 1)
                act.activation(hT_hi[:, cols], scores[0], ACT.Copy).then_inc(hThi_made, 1)
            peeled(act, B, one_batch)
            act.wait_ge(w_made, 1)
            act.wait_ge(hT_made, B)

            def make_q(v, a):
                if later(v, 2):
                    act.wait_ge(scored, v - 1)
                    act.wait_ge(qlo_made, v - 1)
                cols = bass.ds(v * P, P)
                act.activation(q[:, a, :], hT[:, cols], ACT.Copy, scale=w_d[:, 2:3]).then_inc(q_made, 1)
                act.activation(q_hi[:, a, :], hT[:, cols], ACT.Copy, scale=w_d[:, 2:3]).then_inc(qhi_made, 1)

            def make_prob(v, a):
                act.wait_ge(max_made, v + 1)
                if later(v, 2):
                    act.wait_ge(plo_made, v - 1)
                    act.wait_ge(hi_turned, v - 1)
                act.activation(prob[:, a, :], scores[a], ACT.Exp, bias=neg_max[:, a:a + 1],
                               accum_out=row_sum[:, bass.ds(v, 1)]).then_inc(prob_made, 1)
                act.activation(prob_hi[:, a, :], scores[a], ACT.Exp, bias=neg_max[:, a:a + 1]).then_inc(phi_made, 1)

            def step(u, a):
                act.wait_ge(hi_turned, u + 1)
                if later(u, 2):
                    act.wait_ge(attended, u - 1)
                act.activation(probT_hi[:, a, :], turn_hi, ACT.Copy).then_inc(pThi_made, 1)
                if later(u, 2):
                    copy_h2T(u - 2, a)
                if there(u + 2):
                    make_prob(u + 2, a)
                if there(u + 4):
                    make_q(u + 4, a)

            def copy_h2T(v, a):
                act.wait_ge(h2_turned, v + 1)
                if later(v, 2):
                    act.wait_ge(routed, v - 1)
                act.activation(h2_parts[:, v, 0:D], h2[:, a, :], ACT.Copy).then_inc(h2hi_made, 1)
                act.activation(h2T[:, a, :], av_ps[:, a, 2 * D:3 * D], ACT.Copy).then_inc(h2T_made, 1)

            make_q(0, 0)
            make_q(1, 1)
            make_prob(0, 0)
            make_q(2, 0)
            make_prob(1, 1)
            make_q(3, 1)
            run_steps(act, step)
            copy_h2T(NT - 2, 0)
            copy_h2T(NT - 1, 1)

            def one_batch(b):
                act.wait_ge(gap_made, b + 1)
                act.activation(gate2[:, :], gap[:, :], ACT.Exp).then_inc(gate_exp, 1)
            peeled(act, B, one_batch)

            act.wait_ge(small_in, 48)

            def copy_xT(k, a):
                act.wait_ge(xs_turned, k + 1)
                if later(k, NH):
                    act.wait_ge(fc_done, 2 * (k - NH + 1))
                act.activation(xT[:, a % NH, :], bank[a % 2][:, :].bitcast(F16)[:, 0:2 * W], ACT.Copy).then_inc(xT_made, 1)

            def gelu(k, a):
                e = act.value_load(tile_expert[0:1, bass.ds(k, 1)], min_val=0, max_val=E - 1)
                if later(k, NH):
                    act.wait_ge(hid_split, k - NH + 1)
                for c in range(HC):
                    if c % 2 == 0:
                        act.wait_ge(fc_done, k * 2 + c // 2 + 1)
                    act.activation(hid[:, a % NH, c, :], up_ps(a, c), ACT.Gelu_apprx_tanh,
                                   bias=bfc[:, e, c:c + 1], scale=scale_down[:, 0:1]).then_inc(gelu_done, 1)

            def gate(k, a):
                act.wait_ge(biased_made, k + 1)
                if later(k, NB):
                    act.wait_ge(returned[a], 16 * H * (k // NB))
                for h in range(H):
                    ins = act.activation(gated[a][h], biased[:, a % NH, h, :], ACT.Copy, scale=xs[a][:, h, D + 1:D + 2])
                ins.then_inc(gated_made, 1)

            def step(k, a):
                if tile_there(k + 1):
                    copy_xT(k + 1, (a + 1) % NB)
                if tile_there(k):
                    gelu(k, a)
                if later(k, 3):
                    gate(k - 3, (a - 3) % NB)
            act.wait_ge(table_made, 1)
            copy_xT(0, 0)
            run_tiles_ahead(act, step, 3)

        @block.tensor
        def _(pe):
            pe.wait_ge(consts, N_CONSTS)
            def one_batch(b):
                pe.wait_ge(h_made, (b + 1) * BT)
                if later(b):
                    pe.wait_ge(hThi_made, b)
                for t in range(BT):
                    mm = pe.transpose(scores[0][:, t * P:(t + 1) * P], h_tile[:, t, :], ident[:, :])
                mm.then_inc(h_turned, 1)
            peeled(pe, B, one_batch)
            pe.wait_ge(hThi_made, B)
            pe.wait_ge(hTlo_made, B)

            def score(v, a):
                pe.wait_ge(qhi_made, v + 1)
                pe.wait_ge(qlo_made, v + 1)
                if later(v, 2):
                    pe.wait_ge(phi_made, v - 1)
                first = (v // BT) * S
                for n in range(S // 512):
                    cols = bass.ds(first + n * 512, 512)
                    o = scores[a][:, n * 512:(n + 1) * 512]
                    pe.matmul(o, q_hi[:, a, :], hT_hi[:, cols], start=True, stop=False)
                    pe.matmul(o, q_hi[:, a, :], hT_lo[:, cols], start=False, stop=False)
                    mm = pe.matmul(o, q_lo[:, a, :], hT_hi[:, cols], start=False, stop=True)
                mm.then_inc(scored, 1)

            def turn(u, a):
                for parts, to, made, copied, turned in ((prob_hi, turn_hi, phi_made, pThi_made, hi_turned),
                                                        (prob_lo, turn_lo, plo_made, pTlo_made, lo_turned)):
                    pe.wait_ge(made, u + 1)
                    if later(u):
                        pe.wait_ge(copied, u)
                    for t in range(BT):
                        mm = pe.transpose(to[:, t * P:(t + 1) * P], parts[:, a, t * P:(t + 1) * P], ident16[:, :])
                    mm.then_inc(turned, 1)

            def attend(v, a):
                pe.wait_ge(pThi_made, v + 1)
                pe.wait_ge(pTlo_made, v + 1)
                if later(v, 2):
                    pe.wait_ge(att_made, v - 1)
                    pe.wait_ge(logits_out, v - 1)
                first = (v // BT) * BT
                for t in range(BT):
                    pe.matmul(av_ps[:, a, 0:2 * D], probT_hi[:, a, t * P:(t + 1) * P], h_parts[:, first + t, :],
                              start=(t == 0), stop=False, skip_group_check=True)
                    mm = pe.matmul(av_ps[:, a, 0:D], probT_lo[:, a, t * P:(t + 1) * P], h_parts[:, first + t, 0:D],
                                   start=False, stop=(t == BT - 1), skip_group_check=True)
                mm.then_inc(attended, 1)

            def step(u, a):
                if there(u + 2):
                    score(u + 2, a)
                turn(u, a)
                if later(u, 2):
                    turn_h2(u - 2, a)
                if later(u):
                    attend(u - 1, 1 - a)
                if later(u, 2):
                    route(u - 2, a)

            def turn_h2(v, a):
                pe.wait_ge(h2_made, v + 1)
                pe.transpose(av_ps[:, a, 2 * D:3 * D], h2[:, a, :], ident[:, :]).then_inc(h2_turned, 1)

            def route(v, a):
                pe.wait_ge(h2T_made, v + 1)
                pe.matmul(av_ps[:, a, 3 * D:3 * D + E], h2T[:, a, :], rwT[:, :], start=True, stop=True).then_inc(routed, 1)

            pe.wait_ge(hlo_made, B)
            pe.wait_ge(small_in, 48)
            score(0, 0)
            score(1, 1)
            run_steps(pe, step)
            turn_h2(NT - 2, 0)
            attend(NT - 1, 1)
            route(NT - 2, 0)
            turn_h2(NT - 1, 1)
            route(NT - 1, 1)

            def one_batch(b):
                pe.wait_ge(taken_made, b + 1)
                o = av_ps[:, 0, 0:(BT + 1) * E]
                pe.matmul(o, before[:, :], taken[:, :, :].rearrange("p t e -> p (t e)"), start=True, stop=False,
                          skip_group_check=True)
                for t in range(BT):
                    later_tiles = av_ps[:, 0, (t + 1) * E:(BT + 1) * E].rearrange("p (t e) -> p t e", e=E)
                    mm = pe.matmul(later_tiles, ones16[:, :], taken[:, t:t + 1, :].to_broadcast([P, BT - t, E]), start=False,
                                   stop=(t == BT - 1), skip_group_check=True)
                mm.then_inc(ranked, 1)
            peeled(pe, B, one_batch)

            def turn_slots(k, a):
                pe.wait_ge(xs_in[a], 16 * (k // NB + 1))
                if later(k, 2):
                    pe.wait_ge(xT_made, k - 1)
                o = bank[a % 2][:, :].bitcast(F16)
                for part in range(2):
                    for h in range(H):
                        x = xs[a][:, h, :].bitcast(F16)[:, part * D:(part + 1) * D]
                        mm = pe.transpose(o[:, part * W + h * P:part * W + (h + 1) * P], x, ident16[:, :])
                mm.then_inc(xs_turned, 1)

            def up(k, a):
                e = pe.value_load(tile_expert[0:1, bass.ds(k, 1)], min_val=0, max_val=E - 1)
                pe.wait_ge(xT_made, k + 1)
                for c in range(HC):
                    if c % 2 == 0 and later(k, 2):
                        pe.wait_ge(gelu_done, (k - 2) * HC + c + 2)
                    o = up_ps(a, c)
                    w = slice(c * P, (c + 1) * P)
                    pe.matmul(o, wfc_hi[:, e, w], xT[:, a % NH, 0:W], start=True, stop=False, skip_group_check=True)
                    pe.matmul(o, wfc_hi[:, e, w], xT[:, a % NH, W:2 * W], start=False, stop=False, skip_group_check=True)
                    mm = pe.matmul(o, wfc_lo[:, e, w], xT[:, a % NH, 0:W], start=False, stop=True, skip_group_check=True)
                    if c % 2:
                        mm.then_inc(fc_done, 1)

            def down(k, a):
                e = pe.value_load(tile_expert[0:1, bass.ds(k, 1)], min_val=0, max_val=E - 1)
                pe.wait_ge(hid_split, k + 1)
                if later(k, 2):
                    pe.wait_ge(biased_made, k - 1)
                for h in range(H):
                    s = slice(h * P, (h + 1) * P)
                    o = av_ps[:, a % 2, h * 2 * D:(h + 1) * 2 * D]
                    for c in range(HC):
                        pe.matmul(o, hid_hi[:, a % NH, c, s], wpr[:, e, c, :], start=(c == 0), stop=False, skip_group_check=True)
                        mm = pe.matmul(o[:, 0:D], hid_lo[:, a % NH, c, s], wpr[:, e, c, 0:D], start=False, stop=(c == HC - 1), skip_group_check=True)
                mm.then_inc(proj_done, 1)

            def step(k, a):
                if tile_there(k + 1):
                    turn_slots(k + 1, (a + 1) % NB)
                if tile_there(k):
                    up(k, a)
                if later(k, 2):
                    down(k - 2, (a - 2) % NB)

            pe.wait_ge(w_split, 4)
            pe.wait_ge(table_made, 1)
            turn_slots(0, 0)
            run_tiles_ahead(pe, step, 2)

        @block.vector
        def _(dve):
            dve.wait_ge(w_in, 32)
            dve.tensor_tensor(w_d[:, 2:3], w_d[:, 0:1], w_d[:, 1:2], ALU.mult).then_inc(w_made, 1)
            for b in range(B):
                dve.wait_ge(x_in[b], 16)
            def one_batch(b):
                for t in range(BT):
                    ins = dve.bn_stats(stats[:, t, :], res[:, b * BT + t, :])
                ins.then_inc(stats_made, 1)
                wait_apart(dve, stats_made, b + 1)
                for t in range(BT):
                    ins = dve.bn_aggr(moments[:, t, :], stats[:, t, :])
                ins.then_inc(moments_made, 1)
                dve.wait_ge(moments_made, b + 1)
                dve.tensor_scalar(var_eps[:, 0:BT], moments[:, :, 1], EPS, None, ALU.add).then_inc(var_made, 1)
                dve.wait_ge(rstd_made, b + 1)
                if later(b):
                    dve.wait_ge(h_turned, b)
                if later(b):
                    dve.wait_ge(hhi_made, b)
                if later(b):
                    dve.wait_ge(hlo_made, b)
                for t in range(BT):
                    n = b * BT + t
                    dve.tensor_scalar(h_tile[:, t, :], res[:, n, :], moments[:, t, 0:1], rstd[:, t:t + 1],
                                      ALU.subtract, ALU.mult).then_inc(h_made, 1)
                at = bass.ds(b * BT, BT)
                cols = bass.ds(b * S, S)
                dve.wait_ge(hhi_made, b + 1)
                dve.wait_ge(h_made, (b + 1) * BT)
                dve.tensor_tensor(h_parts[:, at, D:2 * D], h_tile[:, :, :], h_parts[:, at, 0:D], ALU.subtract).then_inc(hlo_made, 1)
                dve.wait_ge(hThi_made, b + 1)
                dve.tensor_tensor(hT_lo[:, cols], hT[:, cols], hT_hi[:, cols].bitcast(F32), ALU.subtract).then_inc(hTlo_made, 1)
            peeled(dve, B, one_batch)

            chain = [0]

            def link(ins):
                chain[0] += 1
                ins.then_inc(dve_chain, 1)
                dve.wait_ge(dve_chain, chain[0])

            dve.wait_ge(small_in, 48)
            dve.wait_ge(wfc_in, 16)
            dve.tensor_reduce(peak[:, 0:1], raw_fc[:, :], AX_X, ALU.max, apply_absolute_value=True).then_inc(peak_made, 1)
            dve.wait_ge(wpr_in, 16)
            dve.tensor_reduce(peak[:, 1:2], raw_proj[:, :], AX_X, ALU.max, apply_absolute_value=True).then_inc(peak_made, 1)
            dve.tensor_reduce(peak[:, 2:3], bfc[:, :, :].rearrange("p e c -> p (e c)"), AX_X, ALU.max,
                              apply_absolute_value=True).then_inc(peak_made, 1)
            dve.wait_ge(peaks_made, 1)
            link(dve.scalar_tensor_tensor(out=peaks[:, 2:3], in0=peaks[:, 0:1], scalar=float(D) ** 0.5 * D * 1.01,
                                          in1=peaks[:, 2:3], op0=ALU.mult, op1=ALU.add))
            link(dve.tensor_scalar(peaks[:, 0:3], peaks[:, 0:3], 2.0 ** -90, 2.0 ** 100, ALU.max, ALU.min))
            link(dve.tensor_scalar(pow2[:, :].bitcast(U32), peaks[:, 0:3].bitcast(U32), 0x7F800000, None, ALU.bitwise_and))
            link(dve.reciprocal(scale_up[:, :], pow2[:, :]))
            link(dve.tensor_scalar(scale_up[:, :], scale_up[:, :], TOP, None, ALU.mult))
            link(dve.tensor_scalar(scale_down[:, 0:3], pow2[:, :], 1.0 / TOP, None, ALU.mult))
            link(dve.tensor_tensor(scale_down[:, 3:4], scale_down[:, 1:2], scale_down[:, 2:3], ALU.mult))
            for k, raw, hi, lo in ((0, raw_fc[:, :], wfc_hi[:, :, :].rearrange("p e h -> p (e h)"), wfc_lo[:, :, :].rearrange("p e h -> p (e h)")),
                                   (1, raw_proj[:, :].rearrange("p (e c d) -> p e c d", e=E, c=HC), wpr[:, :, :, 0:D], wpr[:, :, :, D:2 * D])):
                dve.tensor_scalar(hi, raw, scale_up[:, k:k + 1], None, ALU.mult).then_inc(w_split, 1)
                dve.wait_ge(w_split, 2 * k + 1)
                dve.scalar_tensor_tensor(out=lo, in0=raw, scalar=scale_up[:, k:k + 1], in1=hi,
                                         op0=ALU.mult, op1=ALU.subtract).then_inc(w_split, 1)

            def row_max(v, a):
                dve.wait_ge(scored, v + 1)
                if later(v, 2):
                    dve.wait_ge(phi_made, v - 1)
                dve.tensor_reduce(neg_max[:, a:a + 1], scores[a], AX_X, ALU.max, negate=True).then_inc(max_made, 1)

            def finish(v, a):
                dve.wait_ge(prob_made, v + 1)
                dve.reciprocal(inv_sum[:, a:a + 1], row_sum[:, bass.ds(v, 1)]).then_inc(inv_made, 1)
                dve.wait_ge(inv_made, v + 1)
                dve.wait_ge(attended, v + 1)
                dve.scalar_tensor_tensor(out=att[:, a, :], in0=av_ps[:, a, 0:D], scalar=inv_sum[:, a:a + 1],
                                         in1=res[:, v, :], op0=ALU.mult, op1=ALU.add).then_inc(res_made, 1)
                dve.wait_ge(res_made, v + 1)
                dve.scalar_tensor_tensor(out=res[:, v, :], in0=av_ps[:, a, D:2 * D], scalar=inv_sum[:, a:a + 1],
                                         in1=att[:, a, :], op0=ALU.mult, op1=ALU.add).then_inc(att_made, 1)
                wait_apart(dve, att_made, v + 1)
                dve.bn_stats(stats[:, a, :], res[:, v, :]).then_inc(ln2_stats, 1)
                wait_apart(dve, ln2_stats, v + 1)
                dve.bn_aggr(moments[:, a, :], stats[:, a, :]).then_inc(ln2_moments, 1)
                dve.wait_ge(ln2_moments, v + 1)
                dve.tensor_scalar(var2[:, a, :], moments[:, a, 1:2], EPS, None, ALU.add).then_inc(ln2_var, 1)

            def make_h2(v, a):
                dve.wait_ge(ln2_rstd, v + 1)
                if later(v, 2):
                    dve.wait_ge(h2lo_made, v - 1)
                    dve.wait_ge(h2_turned, v - 1)
                dve.tensor_scalar(h2[:, a, :], res[:, v, :], moments[:, a, 0:1], rstd2[:, a, :],
                                  ALU.subtract, ALU.mult).then_inc(h2_made, 1)

            def keep_logits(v, a):
                dve.wait_ge(routed, v + 1)
                dve.tensor_copy(logits[:, v, :], av_ps[:, a, 3 * D:3 * D + E]).then_inc(logits_out, 1)

            def step(u, a):
                if later(u, 3):
                    keep_logits(u - 3, 1 - a)
                if there(u + 2):
                    row_max(u + 2, a)
                if later(u, 2):
                    make_h2(u - 2, a)
                dve.wait_ge(lo_turned, u + 1)
                if later(u, 2):
                    dve.wait_ge(attended, u - 1)
                dve.tensor_copy(probT_lo[:, a, :].bitcast(F32), turn_lo.bitcast(F32)).then_inc(pTlo_made, 1)
                if later(u):
                    finish(u - 1, 1 - a)

            row_max(0, 0)
            row_max(1, 1)
            run_steps(dve, step)
            make_h2(NT - 2, 0)
            keep_logits(NT - 3, 1)
            finish(NT - 1, 1)
            make_h2(NT - 1, 1)
            keep_logits(NT - 2, 0)
            keep_logits(NT - 1, 1)

            def bc(ap):
                return ap.unsqueeze(2).to_broadcast([P, BT, E])

            dve.wait_ge(consts, N_CONSTS)
            dve.wait_ge(h2lo_made, NT)
            LINKS = 18

            def one_batch(b):
                done = [0]

                def link(ins):
                    done[0] += 1
                    ins.then_inc(route_chain, 1)
                    dve.wait_ge(route_chain, b * LINKS + done[0])

                at = bass.ds(b * BT, BT)
                dve.wait_ge(logits_out, NT)
                link(dve.tensor_copy(lg[:, :, :], logits[:, at, :]))
                for k in range(K):
                    p = pick[k]
                    link(dve.tensor_reduce(best[:, :, k], lg[:, :, :], AX_X, ALU.max))
                    link(dve.tensor_tensor(p[:, :, :], lg[:, :, :], bc(best[:, :, k]), ALU.is_equal))
                    link(dve.scalar_tensor_tensor(out=p[:, :, :], in0=p[:, :, :], scalar=-2.0 * E, in1=expert_id[:, :, :],
                                                  op0=ALU.mult, op1=ALU.add))
                    link(dve.tensor_reduce(first_id[:, :], p[:, :, :], AX_X, ALU.min))
                    link(dve.tensor_tensor(p[:, :, :], p[:, :, :], bc(first_id[:, :]), ALU.is_equal))
                    if k == 0:
                        link(dve.scalar_tensor_tensor(out=lg[:, :, :], in0=p[:, :, :], scalar=-3e38, in1=lg[:, :, :],
                                                      op0=ALU.mult, op1=ALU.add))
                dve.tensor_tensor(taken[:, 0:BT, :], pick[0][:, :, :], pick[1][:, :, :], ALU.add).then_inc(taken_made, 1)
                dve.tensor_tensor(gap[:, :], best[:, :, 1], best[:, :, 0], ALU.subtract).then_inc(gap_made, 1)
                dve.wait_ge(ranked, b + 1)
                dve.tensor_tensor(rank[:, :, :], av_ps[:, 0, 0:BT * E].rearrange("p (t e) -> p t e", e=E),
                                  next_slot[:, :].unsqueeze(1).to_broadcast([P, BT, E]), ALU.add).then_inc(route_chain, 1)
                done[0] += 1
                dve.wait_ge(route_chain, b * LINKS + done[0])
                dve.tensor_tensor(next_slot[:, :], next_slot[:, :], av_ps[:, 0, BT * E:(BT + 1) * E], ALU.add).then_inc(route_chain, 1)
                done[0] += 1
                for k in range(K):
                    link(dve.tensor_tensor(pick[k][:, :, :], pick[k][:, :, :], rank[:, :, :], ALU.mult))
                for k in range(K):
                    ins = dve.tensor_reduce(slot_f[:, :, k], pick[k][:, :, :], AX_X, ALU.add)
                ins.then_inc(slots_made, 1)
                dve.wait_ge(gate_exp, b + 1)
                link(dve.tensor_scalar(gate_sum[:, :], gate2[:, :], 1.0, None, ALU.add))
                link(dve.reciprocal(gates[:, :, 0], gate_sum[:, :]))
                dve.tensor_tensor(gates[:, :, 1], gates[:, :, 0], gate2[:, :], ALU.mult).then_inc(slots_made, 1)
                dve.wait_ge(slots_made, 4 * b + 2)
                dve.tensor_copy(slot[:, at, :], slot_f[:, :, :]).then_inc(slots_made, 1)
                dve.tensor_copy(meta[:, at, :, 1], gates[:, :, :]).then_inc(slots_made, 1)
                dve.wait_ge(slots_made, 4 * b + 4)
                assert done[0] == LINKS, done[0]

                def two_tiles(i):
                    for a in range(2):
                        n = b * BT + i * 2 + a
                        if later(n, 2):
                            dve.wait_ge(dispatched[a], 16 * K * (n // 2))
                        dve.tensor_copy(stage[a][:, :, D:ROW], meta[:, n, :, :]).then_inc(stage_made, 1)
                        dve.tensor_copy(stage_slot[a][:, :], slot[:, n, :]).then_inc(stage_made, 1)
                        dve.tensor_copy(stage[a][:, :, :].bitcast(F16)[:, :, 0:2 * D],
                                        h2_parts[:, n, :].unsqueeze(1).to_broadcast([P, K, 2 * D])).then_inc(stage_made, 1)
                peeled(dve, BT // 2, two_tiles)
            peeled(dve, B, one_batch)

            dve.wait_ge(route_chain, B * LINKS)
            link(dve.tensor_tensor(count[:, :], next_slot[:, :], region[:, :], ALU.subtract))
            link(dve.tensor_scalar(tiles[:, :], count[:, :], float(W - 1), None, ALU.add))
            link(dve.tensor_copy(tiles_i[:, :], tiles[:, :]))
            link(dve.tensor_scalar(tiles_i[:, :], tiles_i[:, :], W.bit_length() - 1, None, ALU.logical_shift_right))
            link(dve.tensor_copy(ends[0][:, :], tiles_i[:, :]))
            for i in range(3):
                w = 1 << i
                link(dve.tensor_copy(ends[i + 1][:, 0:w], ends[i][:, 0:w]))
                link(dve.tensor_tensor(ends[i + 1][:, w:E], ends[i][:, w:E], ends[i][:, 0:E - w], ALU.add))
            link(dve.tensor_scalar(last_row[:, :], count[:, :], float(-W), 0.0, ALU.add, ALU.max))

            def over(ap):
                return ap.unsqueeze(1).to_broadcast([P, NTILES, E])

            def per(ap):
                return ap.unsqueeze(2).to_broadcast([P, NTILES, E])

            link(dve.tensor_tensor(past[:, :, :], per(tile_id[:, :]), over(ends[3][:, :]), ALU.is_ge))
            link(dve.tensor_reduce(of_expert[:, :], past[:, :, :], AX_X, ALU.add))
            link(dve.tensor_tensor(past2[:, :, :], past[:, :, :], over(ends[0][:, :]), ALU.mult))
            link(dve.tensor_reduce(tile_row[:, :], past2[:, :, :], AX_X, ALU.add))
            link(dve.tensor_scalar(of_expert[:, :], of_expert[:, :], float(E - 1), None, ALU.min))
            link(dve.tensor_tensor(tile_row[:, :], tile_id[:, :], tile_row[:, :], ALU.subtract))
            link(dve.tensor_tensor(expert_row[:, :, :], per(of_expert[:, :]), over(expert_id[:, 0, :]), ALU.is_equal))
            link(dve.tensor_tensor(expert_row[:, :, :], expert_row[:, :, :], over(last_row[:, :]), ALU.mult))
            link(dve.tensor_reduce(tile_last[:, :], expert_row[:, :, :], AX_X, ALU.add))
            link(dve.tensor_scalar(tile_row[:, :], tile_row[:, :], float(W), None, ALU.mult))
            link(dve.tensor_tensor(tile_last[:, :], tile_row[:, :], tile_last[:, :], ALU.min))
            link(dve.tensor_tensor(skipped[:, :], tile_row[:, :], tile_last[:, :], ALU.subtract))
            link(dve.tensor_scalar(tile_row[:, :], tile_id[:, :], ends[3][:, E - 1:E], float(W), ALU.is_ge, ALU.mult))
            link(dve.tensor_tensor(skipped[:, :], skipped[:, :], tile_row[:, :], ALU.add))
            link(dve.tensor_tensor(spare_row[:, :, :], skipped[:, :].unsqueeze(2).to_broadcast([P, NTILES, H]),
                                   place[:, :].unsqueeze(1).to_broadcast([P, NTILES, H]), ALU.is_gt))
            link(dve.tensor_tensor(spare_row[:, :, :], spare_row[:, :, :], spare[:, :, :], ALU.mult))
            link(dve.scalar_tensor_tensor(out=tile_row[:, :], in0=of_expert[:, :], scalar=float(N), in1=tile_last[:, :],
                                          op0=ALU.mult, op1=ALU.add))
            link(dve.tensor_copy(tile_expert[:, :], of_expert[:, :]))
            dve.tensor_copy(tile_start[:, :], tile_row[:, :]).then_inc(table_made, 1)
            dve.wait_ge(table_made, 1)
            dve.wait_ge(w_split, 4)

            def keep_rows(k, a):
                dve.wait_ge(xs_in[a], 16 * (k // NB + 1))
                if later(k, NB):
                    dve.wait_ge(returned[a], 16 * H * (k // NB))
                dve.tensor_tensor(result_row[a][:, :], xs[a][:, :, D], spare_row[:, k, :], ALU.max).then_inc(row_made, 1)

            def split_hidden(k, a):
                dve.wait_ge(gelu_done, (k + 1) * HC)
                if later(k, NH):
                    dve.wait_ge(proj_done, k - NH + 1)
                h = hid[:, a % NH, :, :].rearrange("p c n -> p (c n)")
                hi = hid_hi[:, a % NH, :, :].rearrange("p c n -> p (c n)")
                lo = hid_lo[:, a % NH, :, :].rearrange("p c n -> p (c n)")
                dve.tensor_scalar(hi, h, scale_up[:, 2:3], None, ALU.mult).then_inc(split_hi, 1)
                dve.wait_ge(split_hi, k + 1)
                dve.scalar_tensor_tensor(out=lo, in0=h, scalar=scale_up[:, 2:3], in1=hi,
                                         op0=ALU.mult, op1=ALU.subtract).then_inc(hid_split, 1)

            def add_bias(k, a):
                e = dve.value_load(tile_expert[0:1, bass.ds(k, 1)], min_val=0, max_val=E - 1)
                dve.wait_ge(proj_done, k + 1)
                if later(k, NH):
                    dve.wait_ge(gated_made, k - NH + 1)
                o = av_ps[:, a % 2, :].rearrange("p (h s d) -> p h s d", h=H, s=2)
                y = biased[:, a % NH, :, :]
                dve.scalar_tensor_tensor(out=y, in0=o[:, :, 0, :], scalar=scale_down[:, 3:4],
                                         in1=bpr[:, bass.ds(e, 1), :].to_broadcast([P, H, D]), op0=ALU.mult, op1=ALU.add).then_inc(bias_added, 1)
                dve.wait_ge(bias_added, k + 1)
                dve.scalar_tensor_tensor(out=y, in0=o[:, :, 1, :], scalar=scale_down[:, 3:4],
                                         in1=y, op0=ALU.mult, op1=ALU.add).then_inc(biased_made, 1)

            def step(k, a):
                if tile_there(k):
                    keep_rows(k, a)
                if later(k, 2):
                    add_bias(k - 2, (a - 2) % NB)
                if tile_there(k):
                    split_hidden(k, a)
            run_tiles(dve, step, 2)

            for b in range(B):
                r = res[:, b * BT:(b + 1) * BT, :]
                half = (raw_fc, raw_proj)[b // 2][:, :].rearrange("p (t k d) -> p t k d", k=K, d=D)
                both = half[:, (b % 2) * BT:(b % 2 + 1) * BT, :, :]
                dve.wait_ge(results_in[b], 16)
                dve.tensor_tensor(r, r, both[:, :, 0, :], ALU.add).then_inc(summed, 1)
                dve.wait_ge(summed, b + 1)
                dve.tensor_tensor(r, r, both[:, :, 1, :], ALU.add).then_inc(added, 1)


_INS = ['L0_attn_x', 'L0_attn_w_lhs', 'L0_attn_w_rhs', 'L0_ffn_router_w', 'L0_ffn_w_fc', 'L0_ffn_b_fc',
        'L0_ffn_w_proj', 'L0_ffn_b_proj']


def kernel(**inputs):
    import numpy as _np
    import concourse.bacc as _bacc
    from concourse import mybir as _mybir
    from concourse.bass_utils import run_bass_kernel_spmd as _run

    x, w_lhs, w_rhs, router_w, w_fc, b_fc, w_proj, b_proj = (_np.asarray(inputs[n]) for n in _INS)
    n_b, n_s, d = x.shape
    n_e, _, hid = w_fc.shape
    laid = {
        "x": x.reshape(n_b * n_s // 128, 128, d).transpose(1, 0, 2),
        "w_lhs": w_lhs.reshape(d, 1),
        "w_rhs": w_rhs.reshape(d, 1),
        "router_wT": router_w.T,
        "w_fc": w_fc.transpose(1, 0, 2),
        "b_fc": b_fc.reshape(n_e, hid // 128, 128).transpose(2, 0, 1),
        "w_proj": w_proj.reshape(n_e, hid // 128, 128, d).transpose(2, 0, 1, 3),
        "b_proj": b_proj,
    }
    nc = _bacc.Bacc("TRN2", target_bir_lowering=False, num_devices=1)
    arrays, args = {}, []
    for name, a in laid.items():
        a = _np.ascontiguousarray(a)
        arrays[f"in_{name}_dram"] = a
        args.append(nc.dram_tensor(f"in_{name}_dram", a.shape, _mybir.dt.from_np(a.dtype), kind="ExternalInput").ap())
    out = nc.dram_tensor("out_0_dram", laid["x"].shape, _mybir.dt.float32, kind="ExternalOutput").ap()
    preln_attention_moe(nc, *args, out)
    r = _run(nc, [arrays], core_ids=[0])
    got = r.results[0]["out_0_dram"]
    return _np.ascontiguousarray(got.transpose(1, 0, 2)).reshape(n_b, n_s, d)
```

```python
from contextlib import ExitStack

import concourse.bass as bass
from concourse import mybir

P = 128
F32 = mybir.dt.float32
F32R = mybir.dt.float32r
F16 = mybir.dt.float16
U32 = mybir.dt.uint32
I32 = mybir.dt.int32
ALU = mybir.AluOpType
ACT = mybir.ActivationFunctionType
AX_X = mybir.AxisListType.X
RMAX = bass.bass_isa.ReduceOp.max
EPS = 1e-5
TOP = 2.0 ** 14


def preln_attention_moe(nc, x, w_lhs, w_rhs, router_wT, w_fc, b_fc, w_proj, b_proj, out):
    NT = x.shape[1]
    D = x.shape[2]
    E = router_wT.shape[1]
    HID = w_fc.shape[2]
    HC = HID // P
    B = 4
    BT = NT // B
    S = BT * P
    N = NT * P
    K = 2
    ROW = D + 2
    H = 2
    W = H * P
    NB = 8
    NTILES = -(-((K * N + E * (W - 1)) // W) // NB) * NB
    EARLY = ((K * (N - S) - E * (W - 1)) // W) // NB * NB
    assert EARLY == 2 * NB
    NH = 4
    slots = nc.dram_tensor("slots", [E * N, ROW], F32, kind="Internal").ap()
    SPARE = K * N + E * W
    results = nc.dram_tensor("results", [SPARE + NTILES * W, D], F32, kind="Internal").ap()
    assert D == P and NT % (B * 8) == 0 and E == 8

    with ExitStack() as ctx:
        def sb(name, shape, dt):
            return ctx.enter_context(nc.sbuf_tensor(name, shape, dt))

        def sem(name):
            return ctx.enter_context(nc.semaphore(name))

        res = sb("res", [P, NT, D], F32)
        h_parts = sb("h_parts", [P, NT, 2 * D], F16)
        hT = sb("hT", [P, NT * P], F32)
        hT_hi = sb("hT_hi", [P, NT * P], F32R)
        hT_lo = sb("hT_lo", [P, NT * P], F32R)
        q_hi = sb("q_hi", [P, 2, P], F32R)
        q_lo = sb("q_lo", [P, 2, P], F32R)
        prob = sb("prob", [P, 2, S], F32)
        h_tile = prob[:, :, :].rearrange("p a (t d) -> p a t d", d=D)
        prob_hi = sb("prob_hi", [P, 2, S], F16)
        prob_lo = sb("prob_lo", [P, 2, S], F16)
        probT_hi = sb("probT_hi", [P, 2, S], F16)
        probT_lo = sb("probT_lo", [P, 2, S], F16)
        neg_max = sb("neg_max", [P, 2], F32)
        row_sum = sb("row_sum", [P, NT], F32)
        inv_sum = sb("inv_sum", [P, 2], F32)
        att = sb("att", [P, 2, D], F32)
        w_d = sb("w_d", [P, 3], F32)
        ident = sb("ident", [P, P], F32)
        ident16 = sb("ident16", [P, P], F16)
        stats = sb("stats", [P, 2, BT, 6], F32)
        moments = sb("moments", [P, 2, BT, 2], F32)
        var_eps = sb("var_eps", [P, 2, BT], F32)
        rstd = sb("rstd", [P, 2, BT], F32)
        stats2 = sb("stats2", [P, 2, 6], F32)
        moments2 = sb("moments2", [P, 2, 2], F32)
        var2 = sb("var2", [P, 2, 1], F32)
        rstd2 = sb("rstd2", [P, 2, 1], F32)
        minus_half = sb("minus_half", [P, NT], F32)

        h2 = sb("h2", [P, 2, D], F32)
        h2_parts = hT[:, :].bitcast(F16).rearrange("p (t d) -> p t d", d=2 * D)
        h2T = sb("h2T", [P, 2, P], F32)
        raw_fc = sb("raw_fc", [P, E * HID], F32)
        raw_proj = sb("raw_proj", [P, E * HID], F32)
        wfc_hi = sb("wfc_hi", [P, E, HID], F16)
        wfc_lo = sb("wfc_lo", [P, E, HID], F16)
        wpr = sb("wpr", [P, E, HC, 2 * D], F16)
        bfc = sb("bfc", [P, E, HC], F32)
        bpr = sb("bpr", [P, E, D], F32)
        rwT = sb("rwT", [P, E], F32)
        piece_peak = sb("piece_peak", [P, 2, BT], F32)
        peak = sb("peak", [P, 4], F32)
        peaks = sb("peaks", [P, 4], F32)
        pow2 = sb("pow2", [P, 3], F32)
        scale_up = sb("scale_up", [P, 3], F32)
        scale_down = sb("scale_down", [P, 4], F32)
        logits = sb("logits", [P, NT, E], F32)
        best = sb("best", [P, BT, 2], F32)
        lg = sb("lg", [P, BT, E], F32)
        first_id = sb("first_id", [P, BT], F32)
        expert_id = sb("expert_id", [P, BT, E], F32)
        gap = sb("gap", [P, BT], F32)
        gate2 = sb("gate2", [P, BT], F32)
        gate_sum = sb("gate_sum", [P, BT], F32)
        gates = sb("gates", [P, BT, 2], F32)
        pick = [sb(f"pick{k}", [P, BT, E], F32) for k in range(K)]
        taken = sb("taken", [P, BT + 1, E], F16)
        rank = sb("rank", [P, BT, E], F32)
        slot_f = sb("slot_f", [P, BT, K], F32)
        slot = sb("slot", [P, NT, K], I32)
        next_slot = sb("next_slot", [P, E], F32)
        meta = sb("meta", [P, NT, K, 2], F32)
        before = sb("before", [P, P], F16)
        ones16 = sb("ones16", [P, P], F16)
        stage = [sb(f"stage{a}", [P, K, ROW], F32) for a in range(2)]
        stage_slot = [sb(f"stage_slot{a}", [P, K], I32) for a in range(2)]
        empty = raw_fc[:, 0:E * H * ROW].rearrange("p (e h r) -> p e h r", e=E, h=H)

        wide = sb("wide", [P, NH * H * D], F32)

        region = sb("region", [P, E], F32)
        count = sb("count", [P, E], F32)
        tiles_i = sb("tiles_i", [P, E], I32)
        tiles = sb("tiles", [P, E], F32)
        ends = [sb(f"ends{i}", [P, E], F32) for i in range(4)]
        last_row = sb("last_row", [P, E], F32)
        tile_id = sb("tile_id", [P, NTILES], F32)
        past = sb("past", [P, NTILES, E], F32)
        first = sb("first", [P, E], F32)
        used = sb("used", [P, E], F32)
        offset = sb("offset", [P, E], F32)
        expert_row = sb("expert_row", [P, NTILES, E], F32)
        of_expert = sb("of_expert", [P, NTILES], F32)
        tile_row = sb("tile_row", [P, NTILES], F32)
        tile_last = sb("tile_last", [P, NTILES], F32)
        gelu_ready = sb("gelu_ready", [P, 1], F32)
        digit = sb("digit", [P, NB], F32)
        digits = sb("digits", [P, NTILES // NB, NB], F32)
        turn_number = sb("turn_number", [P, NTILES // NB], F32)
        turn_experts = sb("turn_experts", [P, NTILES // NB], I32)
        tile_start = sb("tile_start", [P, NTILES], I32)
        skipped = sb("skipped", [P, NTILES], F32)
        place = sb("place", [P, H], F32)
        spare = sb("spare", [P, NTILES, H], F32)
        spare_row = sb("spare_row", [P, NTILES, H], F32)

        xs_all = raw_proj[:, 0:NB * H * ROW].rearrange("p (a h r) -> p a h r", a=NB, h=H)
        xs = [xs_all[:, a, :, :] for a in range(NB)]
        xT = sb("xT", [P, NH, 2 * W], F16)
        hid = raw_fc[:, :].rearrange("p (a c n) -> p a c n", a=NH, c=HC)
        hid_hi = h_parts[:, 0:NT // 2, :].rearrange("p t d -> p (t d)").rearrange("p (a c n) -> p a c n", a=NH, c=HC)
        hid_lo = h_parts[:, NT // 2:NT, :].rearrange("p t d -> p (t d)").rearrange("p (a c n) -> p a c n", a=NH, c=HC)
        biased = wide[:, :].rearrange("p (a h d) -> p a h d", a=NH, h=H)
        gated_all = prob[:, :, :].rearrange("p a s -> p (a s)").rearrange("p (a h d) -> p a h d", a=NB, h=H)
        gated = [[gated_all[:, a, h, :] for h in range(H)] for a in range(NB)]
        result_row = [sb(f"result_row{a}", [P, H], I32) for a in range(NB)]

        bank = [ctx.enter_context(nc.psum_tensor(f"bank{i}", [P, 512], F32)) for i in range(2)]
        sc_ps = ctx.enter_context(nc.psum_tensor("sc_ps", [P, 4, 512], F32))
        av_ps = ctx.enter_context(nc.psum_tensor("av_ps", [P, 2, 512], F32))
        scores = [sc_ps[:, 2 * a:2 * a + 2, :].rearrange("p a n -> p (a n)") for a in range(2)]
        turn_hi = bank[0][:, :].bitcast(F16)
        turn_lo = bank[1][:, :].bitcast(F16)

        x_in = [sem(f"x_in{i}") for i in range(B)]
        small_in = sem("small_in")
        w_in = sem("w_in")
        wfc_in = sem("wfc_in")
        piece_peaks = sem("piece_peaks")
        wpr_scaled = sem("wpr_scaled")
        wprhi_made = sem("wprhi_made")
        wpr_split = sem("wpr_split")
        wpr_in = sem("wpr_in")
        consts = sem("consts")
        stats_made = sem("stats_made")
        moments_made = sem("moments_made")
        var_made = sem("var_made")
        rstd_made = sem("rstd_made")
        h_made = sem("h_made")
        hhi_made = sem("hhi_made")
        hlo_made = sem("hlo_made")
        h_turned = sem("h_turned")
        hT_made = sem("hT_made")
        hThi_made = sem("hThi_made")
        hTlo_made = sem("hTlo_made")
        w_made = sem("w_made")
        whi_made = sem("whi_made")
        scales_made = sem("scales_made")
        ranks_made = sem("ranks_made")
        ranks_kept = sem("ranks_kept")
        qhi_made = sem("qhi_made")
        qlo_made = sem("qlo_made")
        scored = sem("scored")
        max_made = sem("max_made")
        prob_made = sem("prob_made")
        phi_made = sem("phi_made")
        plo_made = sem("plo_made")
        hi_turned = sem("hi_turned")
        lo_turned = sem("lo_turned")
        pThi_made = sem("pThi_made")
        pTlo_made = sem("pTlo_made")
        attended = sem("attended")
        inv_made = sem("inv_made")
        att_made = sem("att_made")
        res_made = sem("res_made")
        ln2_stats = sem("ln2_stats")
        ln2_moments = sem("ln2_moments")
        ln2_var = sem("ln2_var")
        ln2_rstd = sem("ln2_rstd")
        h2_made = sem("h2_made")
        h2hi_made = sem("h2hi_made")
        h2lo_made = sem("h2lo_made")
        h2_turned = sem("h2_turned")
        h2T_made = sem("h2T_made")
        routed = sem("routed")
        logits_out = sem("logits_out")
        gap_made = sem("gap_made")
        waited_apart = sem("waited_apart")
        peak_made = sem("peak_made")
        peaks_made = sem("peaks_made")
        dve_chain = sem("dve_chain")
        route_chain = sem("route_chain")
        gate_exp = sem("gate_exp")
        w_split = sem("w_split")
        taken_made = sem("taken_made")
        ranked = sem("ranked")
        slots_made = sem("slots_made")
        empty_made = sem("empty_made")
        stage_made = sem("stage_made")
        dispatched = [sem(f"dispatched{a}") for a in range(2)]
        table_made = sem("table_made")
        xs_in = [sem(f"xs_in{a}") for a in range(NB)]
        xs_turned = sem("xs_turned")
        xT_made = sem("xT_made")
        fc_done = sem("fc_done")
        gelu_done = sem("gelu_done")
        split_hi = sem("split_hi")
        hid_split = sem("hid_split")
        proj_done = sem("proj_done")
        bias_added = sem("bias_added")
        biased_made = sem("biased_made")
        gated_made = sem("gated_made")
        row_made = sem("row_made")
        returned = [sem(f"returned{a}") for a in range(NB)]
        results_in = [sem(f"results_in{b}") for b in range(B)]
        summed = sem("summed")
        added = sem("added")
        stored = sem("stored")

        N_CONSTS = 17

        block = ctx.enter_context(nc.Block())

        LAG = BT + 4
        assert NT - LAG == 2 * BT + 4

        def run_steps(eng, step):
            for u in range(LAG):
                step(u, u % 2, u % BT, u // BT)
            with eng.Fori(0, 2) as i:
                for j in range(BT):
                    at = (LAG + j) % BT
                    step(LAG + BT * i + j, j % 2, at, i + (LAG + j) // BT)
            for u in range(LAG + 2 * BT, NT):
                step(u, u % 2, u % BT, u // BT)

        PIECES = BT

        def piece(i):
            if i < PIECES:
                return (raw_fc[:, i * HID:(i + 1) * HID], wfc_hi[:, i, :], wfc_lo[:, i, :], 0)
            e = i - PIECES
            return (raw_proj[:, e * HID:(e + 1) * HID].rearrange("p (c d) -> p c d", c=HC), wpr[:, e, :, 0:D], wpr[:, e, :, D:2 * D], 1)

        def over(ap, n):
            return ap.unsqueeze(1).to_broadcast([P, n, E])

        def per(ap, n):
            return ap.unsqueeze(2).to_broadcast([P, n, E])

        def make_table(eng, link, settle, early, parts=(0, 1)):
            of = slice(0, EARLY) if early else slice(EARLY, NTILES)
            n = of.stop - of.start
            k_, e_, row, last = tile_id[:, of], of_expert[:, of], tile_row[:, of], tile_last[:, of]
            if 0 in parts:
                link(eng.tensor_tensor(count[:, :], next_slot[:, :], region[:, :], ALU.subtract))
                yield
                settle()
                link(eng.tensor_scalar(tiles[:, :], count[:, :], 0.0 if early else float(W - 1), None, ALU.add))
                yield
                settle()
                link(eng.tensor_copy(tiles_i[:, :], tiles[:, :]))
                yield
                settle()
                link(eng.tensor_scalar(tiles_i[:, :], tiles_i[:, :], W.bit_length() - 1, None, ALU.logical_shift_right))
                yield
                settle()
                link(eng.tensor_copy(tiles[:, :], tiles_i[:, :]))
                yield
                settle()
                if early:
                    link(eng.tensor_copy(ends[0][:, :], tiles[:, :]))
                    yield
                    settle()
                else:
                    link(eng.tensor_tensor(ends[0][:, :], tiles[:, :], used[:, :], ALU.subtract))
                    yield
                    settle()
                link(eng.tensor_scalar(last_row[:, :], count[:, :], float(-W), 0.0, ALU.add, ALU.max))
                yield
                settle()
                for i in range(3):
                    w = 1 << i
                    eng.tensor_copy(ends[i + 1][:, 0:w], ends[i][:, 0:w])
                    link(eng.tensor_tensor(ends[i + 1][:, w:E], ends[i][:, w:E], ends[i][:, 0:E - w], ALU.add))
                    yield
                    settle()
                link(eng.tensor_tensor(first[:, :], ends[3][:, :], ends[0][:, :], ALU.subtract))
                yield
                settle()
            if 1 in parts:
                link(eng.tensor_tensor(past[:, of, :], per(k_, n), over(ends[3][:, :], n), ALU.is_ge))
                yield
                settle()
                if early:
                    link(eng.tensor_scalar(offset[:, :], first[:, :], float(-W), None, ALU.mult))
                    yield
                    settle()
                else:
                    link(eng.tensor_tensor(offset[:, :], used[:, :], first[:, :], ALU.subtract))
                    yield
                    settle()
                    link(eng.tensor_scalar(offset[:, :], offset[:, :], float(W), None, ALU.mult))
                    yield
                    settle()
                link(eng.tensor_reduce(e_, past[:, of, :], AX_X, ALU.add))
                yield
                settle()
                link(eng.tensor_scalar(e_, e_, float(E - 1), None, ALU.min))
                yield
                settle()
                link(eng.tensor_tensor(past[:, of, :], per(e_, n), over(expert_id[:, 0, :], n), ALU.is_equal))
                yield
                settle()
                link(eng.tensor_tensor(expert_row[:, of, :], past[:, of, :], over(offset[:, :], n), ALU.mult))
                yield
                settle()
                link(eng.tensor_tensor(past[:, of, :], past[:, of, :], over(last_row[:, :], n), ALU.mult))
                yield
                settle()
                link(eng.tensor_reduce(row, expert_row[:, of, :], AX_X, ALU.add))
                yield
                settle()
                link(eng.tensor_reduce(last, past[:, of, :], AX_X, ALU.add))
                yield
                settle()
                link(eng.scalar_tensor_tensor(out=row, in0=k_, scalar=float(W), in1=row, op0=ALU.mult, op1=ALU.add))
                yield
                settle()
                link(eng.tensor_tensor(last, row, last, ALU.min))
                yield
                settle()
                link(eng.tensor_tensor(skipped[:, of], row, last, ALU.subtract))
                yield
                settle()
                link(eng.tensor_scalar(row, k_, ends[3][:, E - 1:E], float(W), ALU.is_ge, ALU.mult))
                yield
                settle()
                link(eng.tensor_tensor(skipped[:, of], skipped[:, of], row, ALU.add))
                yield
                settle()
                link(eng.tensor_tensor(spare_row[:, of, :], skipped[:, of].unsqueeze(2).to_broadcast([P, n, H]),
                                       place[:, :].unsqueeze(1).to_broadcast([P, n, H]), ALU.is_gt))
                yield
                settle()
                link(eng.tensor_tensor(spare_row[:, of, :], spare_row[:, of, :], spare[:, of, :], ALU.mult))
                yield
                settle()
                link(eng.scalar_tensor_tensor(out=row, in0=e_, scalar=float(N), in1=last, op0=ALU.mult, op1=ALU.add))
                yield
                settle()
                turns = slice(of.start // NB, of.stop // NB)
                link(eng.tensor_tensor(digits[:, turns, :], e_.rearrange("p (i a) -> p i a", a=NB),
                                       digit[:, :].unsqueeze(1).to_broadcast([P, n // NB, NB]), ALU.mult))
                yield
                settle()
                link(eng.tensor_reduce(turn_number[:, turns], digits[:, turns, :], AX_X, ALU.add))
                yield
                settle()
                link(eng.tensor_copy(turn_experts[:, turns], turn_number[:, turns]))
                yield
                settle()
                if early:
                    link(eng.tensor_scalar(offset[:, :], first[:, :], float(EARLY), None, ALU.min))
                    yield
                    settle()
                    link(eng.tensor_scalar(used[:, :], ends[3][:, :], float(EARLY), None, ALU.min))
                    yield
                    settle()
                    link(eng.tensor_tensor(used[:, :], used[:, :], offset[:, :], ALU.subtract))
                    yield
                    settle()
                eng.tensor_copy(tile_start[:, of], row).then_inc(table_made, 1)

        def pieces_at(u):
            return (u - 2,) if isinstance(u, int) and 2 <= u < 2 + PIECES else ()

        def peeled(eng, count, body):
            body(0)
            with eng.Fori(1, count) as i:
                body(i)

        def wait_apart(eng, sem, value):
            eng.wait_ge(sem, value)
            eng.sem_inc(waited_apart, 1)

        def later(i, least=1):
            return not isinstance(i, int) or i >= least

        def there(u):
            return not isinstance(u, int) or 0 <= u < NT

        def run_tiles(eng, load_experts, step, lag, ahead, between):
            for first in range(0, EARLY, NB):
                load_experts(first)
                for a in range(NB):
                    step(first + a, a)
            between()
            last = NTILES // NB - ahead
            with eng.Fori(EARLY // NB, last) as i:
                load_experts(i * NB)
                for a in range(NB):
                    step(i * NB + a, a)
            for first in range(last * NB, NTILES, NB):
                load_experts(first)
                for a in range(NB):
                    step(first + a, a)
            load_experts(NTILES)
            for k in range(NTILES, NTILES + lag):
                step(k, k % NB)

        DIGIT = E.bit_length() - 1

        def no_experts(first):
            pass

        def expert_loader(engine, of):
            def load_digits(turn):
                return engine.value_load(turn_experts[0:1, bass.ds(turn, 1)], min_val=0, max_val=E ** NB - 1)

            def load_experts(first):
                if isinstance(first, int) and first == NTILES:
                    of.update({-2: of[NB - 2], -1: of[NB - 1]})
                    return
                turn = first // NB
                if isinstance(first, int) and first == 0:
                    digits = {0: load_digits(turn)}
                else:
                    digits = {-1: load_digits(turn - 1), 0: load_digits(turn)}
                for place in range(-2 if -1 in digits else 0, NB):
                    of[place] = (digits[place // NB] >> (DIGIT * (place % NB))) & (E - 1)
            return load_experts

        rank_ps = av_ps[:, 0, 3 * D + E:3 * D + E + (BT + 1) * E]

        def up_ps(a, c):
            return sc_ps[:, 2 * (a % 2) + c // 2, (c % 2) * W:(c % 2 + 1) * W]

        def tile_there(k):
            return not isinstance(k, int) or 0 <= k < NTILES

        @block.sync
        def _(sp):
            sp.dma_start(w_d[:, 0:1], w_lhs).then_inc(w_in, 16)
            sp.dma_start(w_d[:, 1:2], w_rhs).then_inc(w_in, 16)
            for b in range(B):
                sp.dma_start(res[:, b * BT:(b + 1) * BT, :], x[:, b * BT:(b + 1) * BT, :]).then_inc(x_in[b], 16)
            sp.dma_start(rwT[:, :], router_wT).then_inc(small_in, 16)
            sp.dma_start(bfc[:, :, :], b_fc).then_inc(small_in, 16)
            sp.dma_start(bpr[:, :, :], b_proj.unsqueeze(0).to_broadcast([P, E, D])).then_inc(small_in, 16)
            sp.dma_start(raw_fc[:, :], w_fc.rearrange("c e h -> c (e h)")).then_inc(wfc_in, 16)
            sp.dma_start(raw_proj[:, :], w_proj.rearrange("p e c d -> p (e c d)")).then_inc(wpr_in, 16)
            for a in range(2):
                sp.wait_ge(dispatched[a], 16 + 16 * K * ((NT - BT) // 2))
            sp.wait_ge(table_made, 1)

            def all_dispatched():
                for a in range(2):
                    sp.wait_ge(dispatched[a], 16 + 16 * K * (NT // 2))
                sp.wait_ge(table_made, 2)

            def load(k, a):
                start = sp.value_load(tile_start[0:1, bass.ds(k, 1)], min_val=0, max_val=E * N - W)
                if later(k, NB):
                    sp.wait_ge(returned[a], 16 * H * (k // NB))
                sp.dma_start(xs[a], slots[bass.ds(start, W), :].rearrange("(p h) r -> p h r", h=H)).then_inc(xs_in[a], 16)
            run_tiles(sp, no_experts, load, 0, 0, all_dispatched)

            for a in range(NB):
                sp.wait_ge(returned[a], 16 * H * NTILES // NB)
            both = results[0:K * N, :].rearrange("(t p k) d -> p t (k d)", p=P, k=K)
            for b in range(B):
                half = (raw_fc, raw_proj)[b // 2][:, :].rearrange("p (t x) -> p t x", x=K * D)
                sp.dma_start(half[:, (b % 2) * BT:(b % 2 + 1) * BT, :], both[:, b * BT:(b + 1) * BT, :]).then_inc(results_in[b], 16)
            for b in range(B):
                sp.wait_ge(added, b + 1)
                sp.dma_start(out[:, b * BT:(b + 1) * BT, :], res[:, b * BT:(b + 1) * BT, :]).then_inc(stored, 16)
            sp.wait_ge(stored, 16 * B)

        @block.gpsimd
        def _(pool):
            for m in (ident, ident16):
                pool.memset(m[:, :], 0.0).then_inc(consts, 1)
            pool.memset(minus_half[:, :], -0.5).then_inc(consts, 1)
            pool.iota(expert_id[:, :, :], pattern=[[0, BT], [1, E]], base=0, channel_multiplier=0,
                      allow_small_or_imprecise_dtypes=True).then_inc(consts, 1)
            pool.iota(region[:, :], pattern=[[N, E]], base=0, channel_multiplier=0,
                      allow_small_or_imprecise_dtypes=True).then_inc(consts, 1)
            pool.iota(next_slot[:, :], pattern=[[N, E]], base=0, channel_multiplier=0,
                      allow_small_or_imprecise_dtypes=True).then_inc(consts, 1)
            pool.iota(meta[:, :, :, 0], pattern=[[K * P, NT], [1, K]], base=0, channel_multiplier=K,
                      allow_small_or_imprecise_dtypes=True).then_inc(consts, 1)
            for of in (slice(0, EARLY), slice(EARLY, NTILES)):
                pool.iota(tile_id[:, of], pattern=[[1, of.stop - of.start]], base=0, channel_multiplier=0,
                          allow_small_or_imprecise_dtypes=True).then_inc(consts, 1)
            for a in range(NB):
                ins = pool.memset(digit[:, a:a + 1], float(E ** a))
            ins.then_inc(consts, 1)
            pool.iota(place[:, :], pattern=[[1, H]], base=0, channel_multiplier=H,
                      allow_small_or_imprecise_dtypes=True).then_inc(consts, 1)
            pool.iota(spare[:, :, :], pattern=[[W, NTILES], [1, H]], base=SPARE, channel_multiplier=H,
                      allow_small_or_imprecise_dtypes=True).then_inc(consts, 1)
            pool.memset(taken[:, BT:BT + 1, :], 0.0).then_inc(consts, 1)
            pool.memset(ones16[:, :], 1.0).then_inc(consts, 1)
            pool.wait_ge(consts, N_CONSTS - 3)
            pool.affine_select(out=before[:, :], in_=ones16[:, :], compare_op=ALU.is_gt, fill=0.0,
                               base=0, pattern=[[1, P]], channel_multiplier=-1).then_inc(consts, 1)
            for m in (ident, ident16):
                pool.affine_select(out=m[:, :], in_=m[:, :], compare_op=ALU.not_equal, fill=1.0,
                                   base=0, pattern=[[-1, P]], channel_multiplier=1).then_inc(consts, 1)
            def scale(b):
                pool.wait_ge(var_made, b + 1)
                pool.tensor_tensor(rstd[:, b % 2, :], var_eps[:, b % 2, :], minus_half[:, 0:BT], ALU.pow).then_inc(rstd_made, 1)

            scale(0)
            for b in range(B):
                if b + 1 < B:
                    scale(b + 1)
                at = bass.ds(b * BT, BT)
                pool.wait_ge(h_made, (b + 1) * BT)
                pool.wait_ge(hhi_made, b + 1)
                pool.tensor_tensor(h_parts[:, at, D:2 * D], h_tile[:, b % 2, :, :], h_parts[:, at, 0:D], ALU.subtract).then_inc(hlo_made, 1)

            def scale_ln2(v, a):
                pool.wait_ge(ln2_var, v + 1)
                pool.tensor_tensor(rstd2[:, a, :], var2[:, a, :], minus_half[:, 0:1], ALU.pow).then_inc(ln2_rstd, 1)

            def step(u, a, j, b):
                if later(u, 2):
                    scale_ln2(u - 2, a)
                v = u + 1
                if there(v):
                    if later(v, 2):
                        pool.wait_ge(lo_turned, v - 1)
                    pool.wait_ge(phi_made, v + 1)
                    o = 1 - a
                    pool.tensor_tensor(prob_lo[:, o, :], prob[:, o, :], prob_hi[:, o, :], ALU.subtract).then_inc(plo_made, 1)
                if later(u, LAG):
                    dispatch(u - LAG, a)
                if isinstance(u, int) and u in (0, 1, 2):
                    low_part(u + 1)
                if isinstance(u, int) and u == 0:
                    pool.wait_ge(peak_made, 2)
                    pool.partition_all_reduce(peaks[:, 0:3], peak[:, 0:3], P, RMAX).then_inc(peaks_made, 1)
                for i in pieces_at(u - 1):
                    split_low_proj(i)
                if isinstance(u, int) and u == LAG - 4:
                    clear_empty()
                if isinstance(u, int) and u == LAG - 3:
                    number_empty()
                    store_empty(0)
                if isinstance(u, int) and u == LAG - 2:
                    store_empty(1)
                if isinstance(u, int) and u == LAG - 1:
                    for half in range(2):
                        pool.wait_ge(dispatched[half], 16)

            def low_part(b):
                cols = bass.ds(b * S, S)
                pool.wait_ge(hT_made, b + 1)
                pool.tensor_tensor(hT_lo[:, cols], hT[:, cols], hT_hi[:, cols].bitcast(F32), ALU.subtract).then_inc(hTlo_made, 1)

            def split_low_proj(i):
                raw, hi, lo, k = piece(PIECES + i)
                pool.wait_ge(wpr_scaled, i + 1)
                pool.wait_ge(wprhi_made, i + 1)
                pool.tensor_tensor(lo, raw, hi, ALU.subtract).then_inc(wpr_split, 1)

            EMPTY_PIECES = -(-E * H * ROW // HID)

            def clear_empty():
                pool.wait_ge(w_split, EMPTY_PIECES)
                pool.memset(empty, 0.0).then_inc(empty_made, 1)

            def number_empty():
                pool.wait_ge(empty_made, 1)
                pool.iota(empty[:, :, :, D], pattern=[[W, E], [1, H]], base=K * N, channel_multiplier=H,
                          allow_small_or_imprecise_dtypes=True).then_inc(empty_made, 1)

            def store_empty(half):
                pool.wait_ge(empty_made, 2)
                first = slots.rearrange("(e n) r -> e n r", e=E)[:, 0:W, :].rearrange("e (p h) r -> p e (h r)", h=H)
                of = slice(half * E // 2, (half + 1) * E // 2)
                pool.dma_start(first[:, of, :], empty[:, of, :, :].rearrange("p e h r -> p e (h r)")).then_inc(dispatched[half], 16)

            def dispatch(n, a):
                wait_apart(pool, stage_made, 3 * (n + 1))
                for k in range(K):
                    pool.indirect_dma_start(out=slots[:, :], out_offset=bass.IndirectOffsetOnAxis(ap=stage_slot[a][:, k:k + 1], axis=0),
                                            in_=stage[a][:, k, :], in_offset=None).then_inc(dispatched[a], 16)

            step(-1, 1, -1, 0)
            run_steps(pool, step)
            dispatch(NT - LAG, 0)
            scale_ln2(NT - 2, 0)
            dispatch(NT - LAG + 1, 1)
            scale_ln2(NT - 1, 1)
            for n in range(NT - LAG + 2, NT - BT + 2):
                dispatch(n, n % 2)


            def give_back(k, a):
                pool.wait_ge(row_made, k + 1)
                wait_apart(pool, gated_made, k + 1)
                for h in range(H):
                    pool.indirect_dma_start(out=results[:, :], out_offset=bass.IndirectOffsetOnAxis(ap=result_row[a][:, h:h + 1], axis=0),
                                            in_=gated[a][h], in_offset=None).then_inc(returned[a], 16)

            def step(k, a):
                if isinstance(k, int) and k < BT - 2:
                    dispatch(NT - BT + 2 + k, a % 2)
                if later(k, 3):
                    give_back(k - 3, (a - 3) % NB)
            run_tiles(pool, no_experts, step, 3, 0, lambda: None)

        @block.scalar
        def _(act):
            for b in range(B):
                at = bass.ds(b * BT, BT)
                cols = bass.ds(b * S, S)
                act.wait_ge(h_made, (b + 1) * BT)
                act.activation(h_parts[:, at, 0:D], h_tile[:, b % 2, :, :], ACT.Copy).then_inc(hhi_made, 1)
                act.wait_ge(h_turned, b + 1)
                act.activation(hT_hi[:, cols], scores[b % 2], ACT.Copy).then_inc(hThi_made, 1)
                act.activation(hT[:, cols], scores[b % 2], ACT.Copy).then_inc(hT_made, 1)
            act.wait_ge(w_made, 1)
            act.wait_ge(hT_made, B)

            def make_q(v, a):
                if later(v, 2):
                    act.wait_ge(scored, v - 1)
                    act.wait_ge(qlo_made, v - 1)
                cols = bass.ds(v * P, P)
                act.activation(q_hi[:, a, :], hT[:, cols], ACT.Copy, scale=w_d[:, 2:3]).then_inc(qhi_made, 1)

            def make_prob(v, a):
                act.wait_ge(max_made, v + 1)
                if isinstance(v, int) and v < 2:
                    act.wait_ge(hlo_made, B)
                    act.wait_ge(h_turned, B)
                if later(v, 2):
                    act.wait_ge(plo_made, v - 1)
                    act.wait_ge(hi_turned, v - 1)
                act.activation(prob[:, a, :], scores[a], ACT.Exp, bias=neg_max[:, a:a + 1],
                               accum_out=row_sum[:, bass.ds(v, 1)]).then_inc(prob_made, 1)

            def make_prob_hi(v, a):
                act.activation(prob_hi[:, a, :], scores[a], ACT.Exp, bias=neg_max[:, a:a + 1]).then_inc(phi_made, 1)

            def step(u, a, j, b):
                act.wait_ge(hi_turned, u + 1)
                if later(u, 2):
                    act.wait_ge(attended, u - 1)
                act.activation(probT_hi[:, a, :], turn_hi, ACT.Copy).then_inc(pThi_made, 1)
                if there(u + 2):
                    make_prob(u + 2, a)
                if later(u, 2):
                    copy_h2T(u - 2, a)
                if there(u + 2):
                    make_prob_hi(u + 2, a)
                if there(u + 4):
                    make_q(u + 4, a)
                for i in pieces_at(u):
                    split_high(i)
                    split_high_proj(i)
                if later(u, BT) and j == 3:
                    gate_exps(b - 1)

            def split_high(i):
                raw, hi, lo, k = piece(i)
                if i == 0:
                    act.wait_ge(scales_made, 1)
                act.activation(hi, raw, ACT.Copy, scale=scale_up[:, k:k + 1]).then_inc(whi_made, 1)

            def split_high_proj(i):
                raw, hi, lo, k = piece(PIECES + i)
                act.wait_ge(wpr_scaled, i + 1)
                act.activation(hi, raw, ACT.Copy).then_inc(wprhi_made, 1)

            def gate_exps(b):
                act.wait_ge(gap_made, b + 1)
                act.activation(gate2[:, :], gap[:, :], ACT.Exp).then_inc(gate_exp, 1)

            def copy_h2T(v, a):
                act.wait_ge(h2_turned, v + 1)
                if later(v, 2):
                    act.wait_ge(routed, v - 1)
                act.activation(h2_parts[:, v, 0:D], h2[:, a, :], ACT.Copy).then_inc(h2hi_made, 1)
                act.activation(h2T[:, a, :], av_ps[:, a, 2 * D:3 * D], ACT.Copy).then_inc(h2T_made, 1)

            make_q(0, 0)
            make_q(1, 1)
            make_prob(0, 0)
            make_prob_hi(0, 0)
            make_q(2, 0)
            make_prob(1, 1)
            make_prob_hi(1, 1)
            make_q(3, 1)
            run_steps(act, step)
            copy_h2T(NT - 2, 0)
            copy_h2T(NT - 1, 1)

            act.wait_ge(small_in, 48)

            expert = {}

            def copy_xT(k, a):
                act.wait_ge(xs_turned, k + 1)
                if later(k, NH):
                    act.wait_ge(fc_done, 2 * (k - NH + 1))
                act.activation(xT[:, a % NH, :], bank[a % 2][:, :].bitcast(F16)[:, 0:2 * W], ACT.Copy).then_inc(xT_made, 1)

            def gelu(k, a):
                e = expert[a]
                if later(k, NH):
                    act.wait_ge(hid_split, k - NH + 1)
                for c in range(HC):
                    if c % 2 == 0:
                        act.wait_ge(fc_done, k * 2 + c // 2 + 1)
                    act.activation(hid[:, a % NH, c, :], up_ps(a, c), ACT.Gelu_apprx_tanh,
                                   bias=bfc[:, e, c:c + 1], scale=scale_down[:, 0:1]).then_inc(gelu_done, 1)

            def gate(k, a):
                act.wait_ge(biased_made, k + 1)
                if later(k, NB):
                    act.wait_ge(returned[a], 16 * H * (k // NB))
                for h in range(H):
                    ins = act.activation(gated[a][h], biased[:, a % NH, h, :], ACT.Copy, scale=xs[a][:, h, D + 1:D + 2])
                ins.then_inc(gated_made, 1)

            def step(k, a):
                if tile_there(k + 1):
                    copy_xT(k + 1, (a + 1) % NB)
                if tile_there(k):
                    gelu(k, a)
                if later(k, 3):
                    gate(k - 3, (a - 3) % NB)
            act.wait_ge(table_made, 1)
            gate_exps(B - 1)
            act.activation(gelu_ready[:, :], scale_down[:, 0:1], ACT.Gelu_apprx_tanh)
            copy_xT(0, 0)
            run_tiles(act, expert_loader(act, expert), step, 3, 1, lambda: act.wait_ge(table_made, 2))

        @block.tensor
        def _(pe):
            pe.wait_ge(consts, N_CONSTS)
            for b in range(B):
                if b >= 2:
                    pe.wait_ge(hT_made, b - 1)
                for t in range(BT):
                    pe.wait_ge(h_made, b * BT + t + 1)
                    mm = pe.transpose(scores[b % 2][:, t * P:(t + 1) * P], h_tile[:, b % 2, t, :], ident[:, :])
                mm.then_inc(h_turned, 1)
            pe.wait_ge(hT_made, B)

            def score(v, a):
                pe.wait_ge(qhi_made, v + 1)
                pe.wait_ge(qlo_made, v + 1)
                if later(v, 2):
                    pe.wait_ge(phi_made, v - 1)
                first = (v // BT) * S
                for n in range(S // 512):
                    cols = bass.ds(first + n * 512, 512)
                    o = scores[a][:, n * 512:(n + 1) * 512]
                    pe.matmul(o, q_hi[:, a, :], hT_hi[:, cols], start=True, stop=False)
                    pe.matmul(o, q_hi[:, a, :], hT_lo[:, cols], start=False, stop=False)
                    mm = pe.matmul(o, q_lo[:, a, :], hT_hi[:, cols], start=False, stop=True)
                mm.then_inc(scored, 1)

            def turn(u, a):
                for parts, to, made, copied, turned in ((prob_hi, turn_hi, phi_made, pThi_made, hi_turned),
                                                        (prob_lo, turn_lo, plo_made, pTlo_made, lo_turned)):
                    pe.wait_ge(made, u + 1)
                    if later(u):
                        pe.wait_ge(copied, u)
                    for t in range(BT):
                        mm = pe.transpose(to[:, t * P:(t + 1) * P], parts[:, a, t * P:(t + 1) * P], ident16[:, :])
                    mm.then_inc(turned, 1)

            def attend(v, a):
                pe.wait_ge(pThi_made, v + 1)
                pe.wait_ge(pTlo_made, v + 1)
                if later(v, 2):
                    pe.wait_ge(att_made, v - 1)
                    pe.wait_ge(logits_out, v - 1)
                first = (v // BT) * BT
                for t in range(BT):
                    pe.matmul(av_ps[:, a, 0:2 * D], probT_hi[:, a, t * P:(t + 1) * P], h_parts[:, first + t, :],
                              start=(t == 0), stop=False, skip_group_check=True)
                    mm = pe.matmul(av_ps[:, a, 0:D], probT_lo[:, a, t * P:(t + 1) * P], h_parts[:, first + t, 0:D],
                                   start=False, stop=(t == BT - 1), skip_group_check=True)
                mm.then_inc(attended, 1)

            def step(u, a, j, b):
                if there(u + 2):
                    if j == BT - 2:
                        pe.wait_ge(hTlo_made, b + 2)
                    score(u + 2, a)
                if later(u, 3):
                    route(u - 3, 1 - a)
                if later(u, BT) and j == 4:
                    pe.wait_ge(att_made, u - 1)
                    rank_batch(b - 1)
                turn(u, a)
                if later(u):
                    attend(u - 1, 1 - a)
                if later(u, BT) and j == 4:
                    pe.wait_ge(ranks_kept, b)
                if later(u, 2):
                    turn_h2(u - 2, a)

            def rank_batch(b):
                pe.wait_ge(taken_made, b + 1)
                pe.matmul(rank_ps[:, :], before[:, :], taken[:, :, :].rearrange("p t e -> p (t e)"), start=True, stop=False,
                          skip_group_check=True)
                for t in range(BT):
                    later_tiles = rank_ps[:, (t + 1) * E:(BT + 1) * E].rearrange("p (t e) -> p t e", e=E)
                    mm = pe.matmul(later_tiles, ones16[:, :], taken[:, t:t + 1, :].to_broadcast([P, BT - t, E]), start=False,
                                   stop=(t == BT - 1), skip_group_check=True)
                mm.then_inc(ranked, 1)

            def turn_h2(v, a):
                pe.wait_ge(h2_made, v + 1)
                pe.transpose(av_ps[:, a, 2 * D:3 * D], h2[:, a, :], ident[:, :]).then_inc(h2_turned, 1)

            def route(v, a):
                pe.wait_ge(h2T_made, v + 1)
                pe.matmul(av_ps[:, a, 3 * D:3 * D + E], h2T[:, a, :], rwT[:, :], start=True, stop=True).then_inc(routed, 1)

            pe.wait_ge(hlo_made, B)
            pe.wait_ge(hTlo_made, 1)
            pe.wait_ge(small_in, 48)
            score(0, 0)
            score(1, 1)
            run_steps(pe, step)
            route(NT - 3, 1)
            attend(NT - 1, 1)
            turn_h2(NT - 2, 0)
            route(NT - 2, 0)
            turn_h2(NT - 1, 1)
            route(NT - 1, 1)

            expert = {}

            def turn_slots(k, a):
                pe.wait_ge(xs_in[a], 16 * (k // NB + 1))
                if later(k, 2):
                    pe.wait_ge(xT_made, k - 1)
                o = bank[a % 2][:, :].bitcast(F16)
                for part in range(2):
                    for h in range(H):
                        x = xs[a][:, h, :].bitcast(F16)[:, part * D:(part + 1) * D]
                        mm = pe.transpose(o[:, part * W + h * P:part * W + (h + 1) * P], x, ident16[:, :])
                mm.then_inc(xs_turned, 1)

            def up(k, a):
                e = expert[a]
                pe.wait_ge(xT_made, k + 1)
                for c in range(HC):
                    if c % 2 == 0 and later(k, 2):
                        pe.wait_ge(gelu_done, (k - 2) * HC + c + 2)
                    o = up_ps(a, c)
                    w = slice(c * P, (c + 1) * P)
                    pe.matmul(o, wfc_hi[:, e, w], xT[:, a % NH, 0:W], start=True, stop=False, skip_group_check=True)
                    pe.matmul(o, wfc_hi[:, e, w], xT[:, a % NH, W:2 * W], start=False, stop=False, skip_group_check=True)
                    mm = pe.matmul(o, wfc_lo[:, e, w], xT[:, a % NH, 0:W], start=False, stop=True, skip_group_check=True)
                    if c % 2:
                        mm.then_inc(fc_done, 1)

            def down(k, a, of):
                pe.wait_ge(hid_split, k + 1)
                if isinstance(k, int) and k < 2:
                    pe.wait_ge(ranks_kept, B)
                if later(k, 2):
                    pe.wait_ge(biased_made, k - 1)
                for h in range(H):
                    s = slice(h * P, (h + 1) * P)
                    o = av_ps[:, a % 2, h * 2 * D:(h + 1) * 2 * D]
                    for c in range(HC):
                        pe.matmul(o, hid_hi[:, a % NH, c, s], wpr[:, of, c, :], start=(c == 0), stop=False, skip_group_check=True)
                        mm = pe.matmul(o[:, 0:D], hid_lo[:, a % NH, c, s], wpr[:, of, c, 0:D], start=False, stop=(c == HC - 1), skip_group_check=True)
                mm.then_inc(proj_done, 1)

            def step(k, a):
                if tile_there(k + 1):
                    turn_slots(k + 1, (a + 1) % NB)
                if tile_there(k):
                    up(k, a)
                if later(k, 2):
                    down(k - 2, (a - 2) % NB, expert[a - 2])

            pe.wait_ge(w_split, PIECES)
            pe.wait_ge(wpr_split, PIECES)
            pe.wait_ge(table_made, 1)
            rank_batch(B - 1)
            turn_slots(0, 0)
            run_tiles(pe, expert_loader(pe, expert), step, 2, 1, lambda: pe.wait_ge(table_made, 2))

        @block.vector
        def _(dve):
            dve.wait_ge(w_in, 32)
            dve.tensor_tensor(w_d[:, 2:3], w_d[:, 0:1], w_d[:, 1:2], ALU.mult).then_inc(w_made, 1)

            def take_stats(b):
                dve.wait_ge(x_in[b], 16)
                if b >= 2:
                    dve.wait_ge(h_made, (b - 1) * BT)
                for t in range(BT):
                    ins = dve.bn_stats(stats[:, b % 2, t, :], res[:, b * BT + t, :])
                ins.then_inc(stats_made, 1)
                dve.wait_ge(stats_made, b + 1)
                for t in range(BT):
                    ins = dve.bn_aggr(moments[:, b % 2, t, :], stats[:, b % 2, t, :])
                ins.then_inc(moments_made, 1)
                dve.wait_ge(moments_made, b + 1)
                dve.tensor_scalar(var_eps[:, b % 2, :], moments[:, b % 2, :, 1], EPS, None, ALU.add).then_inc(var_made, 1)

            def normalise(b):
                dve.wait_ge(rstd_made, b + 1)
                if b >= 2:
                    dve.wait_ge(h_turned, b - 1)
                    dve.wait_ge(hhi_made, b - 1)
                    dve.wait_ge(hlo_made, b - 1)
                for t in range(BT):
                    dve.tensor_scalar(h_tile[:, b % 2, t, :], res[:, b * BT + t, :], moments[:, b % 2, t, 0:1],
                                      rstd[:, b % 2, t:t + 1], ALU.subtract, ALU.mult).then_inc(h_made, 1)

            def low_part(b):
                cols = bass.ds(b * S, S)
                dve.wait_ge(hT_made, b + 1)
                dve.tensor_tensor(hT_lo[:, cols], hT[:, cols], hT_hi[:, cols].bitcast(F32), ALU.subtract).then_inc(hTlo_made, 1)

            take_stats(0)
            take_stats(1)
            normalise(0)
            take_stats(2)
            normalise(1)
            low_part(0)
            take_stats(3)
            normalise(2)
            normalise(3)

            chain = [0]

            def link(ins):
                chain[0] += 1
                ins.then_inc(dve_chain, 1)
                dve.wait_ge(dve_chain, chain[0])

            def find_peaks(i):
                raw, _, _, k = piece(i)
                flat = (raw_fc, raw_proj)[k][:, (i % PIECES) * HID:(i % PIECES + 1) * HID]
                if i == 0:
                    dve.wait_ge(wfc_in, 16)
                if i == PIECES:
                    dve.wait_ge(wpr_in, 16)
                dve.tensor_reduce(piece_peak[:, k, i % PIECES:i % PIECES + 1], flat, AX_X, ALU.max,
                                  apply_absolute_value=True).then_inc(piece_peaks, 1)

            def join_peaks():
                dve.wait_ge(piece_peaks, 2 * PIECES)
                dve.tensor_reduce(peak[:, 0:2], piece_peak[:, :, :], AX_X, ALU.max).then_inc(peak_made, 1)
                dve.wait_ge(small_in, 48)
                dve.tensor_reduce(peak[:, 2:3], bfc[:, :, :].rearrange("p e c -> p (e c)"), AX_X, ALU.max,
                                  apply_absolute_value=True).then_inc(peak_made, 1)

            def find_scales():
                dve.wait_ge(peaks_made, 1)
                link(dve.scalar_tensor_tensor(out=peaks[:, 2:3], in0=peaks[:, 0:1], scalar=float(D) ** 0.5 * D * 1.01,
                                              in1=peaks[:, 2:3], op0=ALU.mult, op1=ALU.add))
                link(dve.tensor_scalar(peaks[:, 0:3], peaks[:, 0:3], 2.0 ** -90, 2.0 ** 100, ALU.max, ALU.min))
                link(dve.tensor_scalar(pow2[:, :].bitcast(U32), peaks[:, 0:3].bitcast(U32), 0x7F800000, None, ALU.bitwise_and))
                link(dve.reciprocal(scale_up[:, :], pow2[:, :]))
                link(dve.tensor_scalar(scale_up[:, :], scale_up[:, :], TOP, None, ALU.mult))
                dve.sem_inc(scales_made, 1)
                link(dve.tensor_scalar(scale_down[:, 0:3], pow2[:, :], 1.0 / TOP, None, ALU.mult))
                link(dve.tensor_tensor(scale_down[:, 3:4], scale_down[:, 1:2], scale_down[:, 2:3], ALU.mult))

            def scale_proj(i):
                raw, hi, lo, k = piece(PIECES + i)
                dve.tensor_scalar(raw, raw, scale_up[:, k:k + 1], None, ALU.mult).then_inc(wpr_scaled, 1)

            def split_low(i):
                raw, hi, lo, k = piece(i)
                dve.wait_ge(whi_made, i + 1)
                dve.scalar_tensor_tensor(out=lo, in0=raw, scalar=scale_up[:, k:k + 1], in1=hi,
                                         op0=ALU.mult, op1=ALU.subtract).then_inc(w_split, 1)

            def split_q(v, a):
                dve.wait_ge(qhi_made, v + 1)
                dve.scalar_tensor_tensor(out=q_lo[:, a, :], in0=hT[:, bass.ds(v * P, P)], scalar=w_d[:, 2:3],
                                         in1=q_hi[:, a, :].bitcast(F32), op0=ALU.mult, op1=ALU.subtract).then_inc(qlo_made, 1)

            def split_h2(v, a):
                dve.wait_ge(h2hi_made, v + 1)
                dve.tensor_tensor(h2_parts[:, v, D:2 * D], h2[:, a, :], h2_parts[:, v, 0:D], ALU.subtract).then_inc(h2lo_made, 1)

            def row_max(v, a):
                dve.wait_ge(scored, v + 1)
                if later(v, 2):
                    dve.wait_ge(phi_made, v - 1)
                dve.tensor_reduce(neg_max[:, a:a + 1], scores[a], AX_X, ALU.max, negate=True).then_inc(max_made, 1)

            def invert(v, a):
                dve.wait_ge(prob_made, v + 1)
                dve.reciprocal(inv_sum[:, a:a + 1], row_sum[:, bass.ds(v, 1)]).then_inc(inv_made, 1)

            def add_attention(v, a):
                dve.wait_ge(inv_made, v + 1)
                dve.wait_ge(attended, v + 1)
                dve.scalar_tensor_tensor(out=att[:, a, :], in0=av_ps[:, a, 0:D], scalar=inv_sum[:, a:a + 1],
                                         in1=res[:, v, :], op0=ALU.mult, op1=ALU.add).then_inc(res_made, 1)

            def add_attention_low(v, a):
                dve.wait_ge(res_made, v + 1)
                dve.scalar_tensor_tensor(out=res[:, v, :], in0=av_ps[:, a, D:2 * D], scalar=inv_sum[:, a:a + 1],
                                         in1=att[:, a, :], op0=ALU.mult, op1=ALU.add).then_inc(att_made, 1)

            def take_stats2(v, a):
                wait_apart(dve, att_made, v + 1)
                dve.bn_stats(stats2[:, a, :], res[:, v, :]).then_inc(ln2_stats, 1)

            def take_moments2(v, a):
                wait_apart(dve, ln2_stats, v + 1)
                dve.bn_aggr(moments2[:, a, :], stats2[:, a, :]).then_inc(ln2_moments, 1)

            def take_var2(v, a):
                dve.wait_ge(ln2_moments, v + 1)
                dve.tensor_scalar(var2[:, a, :], moments2[:, a, 1:2], EPS, None, ALU.add).then_inc(ln2_var, 1)

            def make_h2(v, a):
                dve.wait_ge(ln2_rstd, v + 1)
                if later(v, 2):
                    dve.wait_ge(h2lo_made, v - 1)
                    dve.wait_ge(h2_turned, v - 1)
                dve.tensor_scalar(h2[:, a, :], res[:, v, :], moments2[:, a, 0:1], rstd2[:, a, :],
                                  ALU.subtract, ALU.mult).then_inc(h2_made, 1)

            def keep_logits(v, a):
                dve.wait_ge(routed, v + 1)
                dve.tensor_copy(logits[:, v, :], av_ps[:, a, 3 * D:3 * D + E]).then_inc(logits_out, 1)

            def bc(ap):
                return ap.unsqueeze(2).to_broadcast([P, BT, E])

            LINKS = 16
            done = [0]

            def route_link(b, ins):
                done[0] += 1
                ins.then_inc(route_chain, 1)
                dve.wait_ge(route_chain, b * LINKS + done[0])

            def note(ins):
                chain[0] += 1
                ins.then_inc(dve_chain, 1)

            def settle():
                dve.wait_ge(dve_chain, chain[0])

            early_table = make_table(dve, note, settle, True)
            PICKS = 12
            LATE_STEPS = 26

            def pick_link(b, n):
                if n:
                    dve.wait_ge(route_chain, b * LINKS + n)
                k = 0 if n < 7 else 1
                p = pick[k]
                if n == 0:
                    ins = dve.tensor_copy(lg[:, :, :], logits[:, bass.ds(b * BT, BT), :])
                elif n in (1, 7):
                    ins = dve.tensor_reduce(best[:, :, k], lg[:, :, :], AX_X, ALU.max)
                elif n in (2, 8):
                    ins = dve.tensor_tensor(p[:, :, :], lg[:, :, :], bc(best[:, :, k]), ALU.is_equal)
                elif n in (3, 9):
                    ins = dve.scalar_tensor_tensor(out=p[:, :, :], in0=p[:, :, :], scalar=-2.0 * E, in1=expert_id[:, :, :],
                                                   op0=ALU.mult, op1=ALU.add)
                elif n in (4, 10):
                    ins = dve.tensor_reduce(first_id[:, :], p[:, :, :], AX_X, ALU.min)
                elif n in (5, 11):
                    ins = dve.tensor_tensor(p[:, :, :], p[:, :, :], bc(first_id[:, :]), ALU.is_equal)
                elif n == 6:
                    ins = dve.scalar_tensor_tensor(out=lg[:, :, :], in0=p[:, :, :], scalar=-3e38, in1=lg[:, :, :],
                                                   op0=ALU.mult, op1=ALU.add)
                else:
                    dve.tensor_tensor(gap[:, :], best[:, :, 1], best[:, :, 0], ALU.subtract).then_inc(gap_made, 1)
                    dve.tensor_tensor(taken[:, 0:BT, :], pick[0][:, :, :], pick[1][:, :, :], ALU.add).then_inc(taken_made, 1)
                    return
                ins.then_inc(route_chain, 1)

            def keep_ranks(b):
                dve.wait_ge(ranked, b + 1)
                dve.tensor_tensor(rank[:, :, :], rank_ps[:, 0:BT * E].rearrange("p (t e) -> p t e", e=E),
                                  next_slot[:, :].unsqueeze(1).to_broadcast([P, BT, E]), ALU.add).then_inc(ranks_made, 1)
                dve.wait_ge(ranks_made, b + 1)
                dve.tensor_tensor(next_slot[:, :], next_slot[:, :], rank_ps[:, BT * E:(BT + 1) * E], ALU.add).then_inc(ranks_kept, 1)

            def find_slots(b):
                at = bass.ds(b * BT, BT)
                done[0] = PICKS
                dve.wait_ge(gate_exp, b + 1)
                route_link(b, dve.tensor_scalar(gate_sum[:, :], gate2[:, :], 1.0, None, ALU.add))
                route_link(b, dve.reciprocal(gates[:, :, 0], gate_sum[:, :]))
                dve.tensor_tensor(gates[:, :, 1], gates[:, :, 0], gate2[:, :], ALU.mult).then_inc(slots_made, 1)
                for k in range(K):
                    route_link(b, dve.tensor_tensor(pick[k][:, :, :], pick[k][:, :, :], rank[:, :, :], ALU.mult))
                for k in range(K):
                    ins = dve.tensor_reduce(slot_f[:, :, k], pick[k][:, :, :], AX_X, ALU.add)
                ins.then_inc(slots_made, 1)
                dve.wait_ge(slots_made, 4 * b + 2)
                dve.tensor_copy(slot[:, at, :], slot_f[:, :, :]).then_inc(slots_made, 1)
                dve.tensor_copy(meta[:, at, :, 1], gates[:, :, :]).then_inc(slots_made, 1)
                if isinstance(b, int):
                    assert done[0] == LINKS, done[0]
                dve.wait_ge(slots_made, 4 * b + 4)

            def fill_stage(n, a):
                dve.wait_ge(dispatched[a], 16 + 16 * K * (n // 2))
                dve.tensor_copy(stage[a][:, :, D:ROW], meta[:, n, :, :]).then_inc(stage_made, 1)
                dve.tensor_copy(stage_slot[a][:, :], slot[:, n, :]).then_inc(stage_made, 1)
                dve.tensor_copy(stage[a][:, :, :].bitcast(F16)[:, :, 0:2 * D],
                                h2_parts[:, n, :].unsqueeze(1).to_broadcast([P, K, 2 * D])).then_inc(stage_made, 1)

            def step(u, a, j, b):
                routed_here = later(u, BT) and j == 2

                def choose(n):
                    if routed_here:
                        pick_link(b - 1, n)
                    if isinstance(u, int) and (u > NT - 4 or u == NT - 4 and n > 4):
                        next(early_table, None)

                if later(u, 3):
                    keep_logits(u - 3, 1 - a)
                if routed_here:
                    dve.wait_ge(logits_out, u - 2)
                choose(0)
                if there(u + 2):
                    row_max(u + 2, a)
                choose(1)
                if later(u, 2):
                    make_h2(u - 2, a)
                if later(u):
                    invert(u - 1, 1 - a)
                if there(u + 3):
                    split_q(u + 3, 1 - a)
                for i in pieces_at(u):
                    scale_proj(i)
                choose(2)
                if later(u, LAG) and j != 4:
                    fill_stage(u - LAG, a)
                choose(3)
                if later(u, 3):
                    split_h2(u - 3, 1 - a)
                choose(4)
                if later(u, BT) and j == 4:
                    keep_ranks(b - 1)
                    find_slots(b - 1)
                    fill_stage(u - LAG, a)
                dve.wait_ge(lo_turned, u + 1)
                if later(u, 2):
                    dve.wait_ge(attended, u - 1)
                dve.tensor_copy(probT_lo[:, a, :].bitcast(F32), turn_lo.bitcast(F32)).then_inc(pTlo_made, 1)
                choose(5)
                if isinstance(u, int) and u == NT - 1:
                    fill_stage(NT - LAG, 0)
                choose(6)
                if later(u):
                    add_attention(u - 1, 1 - a)
                    choose(7)
                    add_attention_low(u - 1, 1 - a)
                    choose(8)
                    take_stats2(u - 1, 1 - a)
                    for i in pieces_at(u - 1):
                        split_low(i)
                    choose(9)
                    take_moments2(u - 1, 1 - a)
                    choose(10)
                    take_var2(u - 1, 1 - a)
                choose(11)
                choose(12)
                if isinstance(u, int) and u == 0:
                    for i in range(11, 2 * PIECES):
                        find_peaks(i)
                    join_peaks()
                if isinstance(u, int) and u == 1:
                    find_scales()

            dve.wait_ge(consts, N_CONSTS)
            split_q(0, 0)
            split_q(1, 1)
            for i in range(5):
                find_peaks(i)
            row_max(0, 0)
            find_peaks(5)
            row_max(1, 1)
            split_q(2, 0)
            for i in range(6, 11):
                find_peaks(i)
            run_steps(dve, step)
            fill_stage(NT - LAG + 1, 1)
            keep_logits(NT - 3, 1)
            make_h2(NT - 2, 0)
            invert(NT - 1, 1)
            add_attention(NT - 1, 1)
            add_attention_low(NT - 1, 1)
            take_stats2(NT - 1, 1)
            take_moments2(NT - 1, 1)
            take_var2(NT - 1, 1)
            split_h2(NT - 3, 1)
            make_h2(NT - 1, 1)
            keep_logits(NT - 2, 0)
            for n in range(NT - LAG + 2, NT - BT):
                fill_stage(n, n % 2)
            split_h2(NT - 2, 0)
            for _ in early_table:
                pass
            keep_logits(NT - 1, 1)
            split_h2(NT - 1, 1)
            dve.wait_ge(logits_out, NT)
            for n in range(PICKS + 1):
                pick_link(B - 1, n)
            keep_ranks(B - 1)
            find_slots(B - 1)
            for n in (NT - BT, NT - BT + 1):
                fill_stage(n, n % 2)
            late_table = make_table(dve, note, settle, False)
            for _ in range(LATE_STEPS):
                next(late_table)

            expert = {}

            def keep_rows(k, a):
                dve.wait_ge(xs_in[a], 16 * (k // NB + 1))
                if later(k, NB):
                    dve.wait_ge(returned[a], 16 * H * (k // NB))
                dve.tensor_tensor(result_row[a][:, :], xs[a][:, :, D], spare_row[:, k, :], ALU.max).then_inc(row_made, 1)

            def split_hidden(k, a):
                dve.wait_ge(gelu_done, (k + 1) * HC)
                if later(k, NH):
                    dve.wait_ge(proj_done, k - NH + 1)
                h = hid[:, a % NH, :, :].rearrange("p c n -> p (c n)")
                hi = hid_hi[:, a % NH, :, :].rearrange("p c n -> p (c n)")
                dve.tensor_scalar(hi, h, scale_up[:, 2:3], None, ALU.mult).then_inc(split_hi, 1)

            def split_hidden_low(k, a):
                h = hid[:, a % NH, :, :].rearrange("p c n -> p (c n)")
                hi = hid_hi[:, a % NH, :, :].rearrange("p c n -> p (c n)")
                lo = hid_lo[:, a % NH, :, :].rearrange("p c n -> p (c n)")
                dve.wait_ge(split_hi, k + 1)
                dve.scalar_tensor_tensor(out=lo, in0=h, scalar=scale_up[:, 2:3], in1=hi,
                                         op0=ALU.mult, op1=ALU.subtract).then_inc(hid_split, 1)

            def add_bias(k, a, of):
                dve.wait_ge(proj_done, k + 1)
                if later(k, NH):
                    dve.wait_ge(gated_made, k - NH + 1)
                o = av_ps[:, a % 2, :].rearrange("p (h s d) -> p h s d", h=H, s=2)
                y = biased[:, a % NH, :, :]
                dve.scalar_tensor_tensor(out=y, in0=o[:, :, 0, :], scalar=scale_down[:, 3:4],
                                         in1=bpr[:, bass.ds(of, 1), :].to_broadcast([P, H, D]), op0=ALU.mult, op1=ALU.add).then_inc(bias_added, 1)

            def add_cross(k, a):
                o = av_ps[:, a % 2, :].rearrange("p (h s d) -> p h s d", h=H, s=2)
                y = biased[:, a % NH, :, :]
                dve.wait_ge(bias_added, k + 1)
                dve.scalar_tensor_tensor(out=y, in0=o[:, :, 1, :], scalar=scale_down[:, 3:4],
                                         in1=y, op0=ALU.mult, op1=ALU.add).then_inc(biased_made, 1)

            def step(k, a):
                if isinstance(k, int) and k < BT - 2:
                    fill_stage(NT - BT + 2 + k, a % 2)
                if isinstance(k, int) and k < BT:
                    for _ in range(2):
                        next(late_table, None)
                if isinstance(k, int) and k == BT:
                    for _ in late_table:
                        pass
                if tile_there(k):
                    keep_rows(k, a)
                if later(k, 2):
                    add_bias(k - 2, (a - 2) % NB, expert[a - 2])
                if tile_there(k):
                    split_hidden(k, a)
                if later(k, 2):
                    add_cross(k - 2, (a - 2) % NB)
                if tile_there(k):
                    split_hidden_low(k, a)
            run_tiles(dve, expert_loader(dve, expert), step, 2, 0, lambda: dve.wait_ge(table_made, 2))

            for b in range(B):
                r = res[:, b * BT:(b + 1) * BT, :]
                half = (raw_fc, raw_proj)[b // 2][:, :].rearrange("p (t k d) -> p t k d", k=K, d=D)
                both = half[:, (b % 2) * BT:(b % 2 + 1) * BT, :, :]
                dve.wait_ge(results_in[b], 16)
                dve.tensor_tensor(r, r, both[:, :, 0, :], ALU.add).then_inc(summed, 1)
                dve.wait_ge(summed, b + 1)
                dve.tensor_tensor(r, r, both[:, :, 1, :], ALU.add).then_inc(added, 1)


_INS = ['L0_attn_x', 'L0_attn_w_lhs', 'L0_attn_w_rhs', 'L0_ffn_router_w', 'L0_ffn_w_fc', 'L0_ffn_b_fc',
        'L0_ffn_w_proj', 'L0_ffn_b_proj']


def kernel(**inputs):
    import numpy as _np
    import concourse.bacc as _bacc
    from concourse import mybir as _mybir
    from concourse.bass_utils import run_bass_kernel_spmd as _run

    x, w_lhs, w_rhs, router_w, w_fc, b_fc, w_proj, b_proj = (_np.asarray(inputs[n]) for n in _INS)
    n_b, n_s, d = x.shape
    n_e, _, hid = w_fc.shape
    laid = {
        "x": x.reshape(n_b * n_s // 128, 128, d).transpose(1, 0, 2),
        "w_lhs": w_lhs.reshape(d, 1),
        "w_rhs": w_rhs.reshape(d, 1),
        "router_wT": router_w.T,
        "w_fc": w_fc.transpose(1, 0, 2),
        "b_fc": b_fc.reshape(n_e, hid // 128, 128).transpose(2, 0, 1),
        "w_proj": w_proj.reshape(n_e, hid // 128, 128, d).transpose(2, 0, 1, 3),
        "b_proj": b_proj,
    }
    nc = _bacc.Bacc("TRN2", target_bir_lowering=False, num_devices=1)
    arrays, args = {}, []
    for name, a in laid.items():
        a = _np.ascontiguousarray(a)
        arrays[f"in_{name}_dram"] = a
        args.append(nc.dram_tensor(f"in_{name}_dram", a.shape, _mybir.dt.from_np(a.dtype), kind="ExternalInput").ap())
    out = nc.dram_tensor("out_0_dram", laid["x"].shape, _mybir.dt.float32, kind="ExternalOutput").ap()
    preln_attention_moe(nc, *args, out)
    r = _run(nc, [arrays], core_ids=[0])
    got = r.results[0]["out_0_dram"]
    return _np.ascontiguousarray(got.transpose(1, 0, 2)).reshape(n_b, n_s, d)
```
